# Optimizing a Trainium2 kernel written in Bass

```python
import numpy as np
import jax
import jax.numpy as jnp

def _softmax(x, axis=-1):
    return jax.nn.softmax(x, axis=axis)

def _gelu(x):
    return jax.nn.gelu(x, approximate=True)

def _silu(x):
    return jax.nn.silu(x)

def _sigmoid(x):
    return jax.nn.sigmoid(x)

def _layernorm(x, axis=-1, eps=1e-05):
    m = jnp.mean(x, axis=axis, keepdims=True)
    v = jnp.var(x, axis=axis, keepdims=True)
    return (x - m) / jnp.sqrt(v + eps)

def _scatter_add(tgt, idx, src, axis=0):
    return tgt.at[idx].add(src)

def _segment_sum(src, seg, n):
    return jax.ops.segment_sum(src, seg, n)
kernel_name = 'mk_rec_standalone_d1_rec_r8_c4306e'

def setup_inputs(seed: int=0):
    np.random.seed(seed)
    _w = jnp.asarray

    def _rec_inputs():
        import jax
        import jax.numpy as jnp
        _rk = jax.random.key(seed)
        r_input_ids = jnp.stack([jax.random.randint(jax.random.fold_in(jax.random.fold_in(_rk, 1), 0), (2048,), 106, 99921, jnp.int32), jax.random.randint(jax.random.fold_in(jax.random.fold_in(_rk, 1), 1), (2048,), 89, 99959, jnp.int32), jax.random.randint(jax.random.fold_in(jax.random.fold_in(_rk, 1), 2), (2048,), 2, 99940, jnp.int32), jax.random.randint(jax.random.fold_in(jax.random.fold_in(_rk, 1), 3), (2048,), 316, 99943, jnp.int32), jax.random.randint(jax.random.fold_in(jax.random.fold_in(_rk, 1), 4), (2048,), 169, 99593, jnp.int32), jax.random.randint(jax.random.fold_in(jax.random.fold_in(_rk, 1), 5), (2048,), 329, 99969, jnp.int32), jax.random.randint(jax.random.fold_in(jax.random.fold_in(_rk, 1), 6), (2048,), 114, 12496, jnp.int32), jax.random.randint(jax.random.fold_in(jax.random.fold_in(_rk, 1), 7), (2048,), 50, 99981, jnp.int32), jax.random.randint(jax.random.fold_in(jax.random.fold_in(_rk, 1), 8), (2048,), 92, 99987, jnp.int32), jax.random.randint(jax.random.fold_in(jax.random.fold_in(_rk, 1), 9), (2048,), 300, 99932, jnp.int32), jax.random.randint(jax.random.fold_in(jax.random.fold_in(_rk, 1), 10), (2048,), 24, 99983, jnp.int32), jax.random.randint(jax.random.fold_in(jax.random.fold_in(_rk, 1), 11), (2048,), 217, 99967, jnp.int32), jax.random.randint(jax.random.fold_in(jax.random.fold_in(_rk, 1), 12), (2048,), 96, 99965, jnp.int32), jax.random.randint(jax.random.fold_in(jax.random.fold_in(_rk, 1), 13), (2048,), 27, 99951, jnp.int32), jax.random.randint(jax.random.fold_in(jax.random.fold_in(_rk, 1), 14), (2048,), 333, 99890, jnp.int32), jax.random.randint(jax.random.fold_in(jax.random.fold_in(_rk, 1), 15), (2048,), 233, 99819, jnp.int32), jax.random.randint(jax.random.fold_in(jax.random.fold_in(_rk, 1), 16), (2048,), 104, 99995, jnp.int32), jax.random.randint(jax.random.fold_in(jax.random.fold_in(_rk, 1), 17), (2048,), 49, 99405, jnp.int32), jax.random.randint(jax.random.fold_in(jax.random.fold_in(_rk, 1), 18), (2048,), 173, 99990, jnp.int32), jax.random.randint(jax.random.fold_in(jax.random.fold_in(_rk, 1), 19), (2048,), 68, 99908, jnp.int32), jax.random.randint(jax.random.fold_in(jax.random.fold_in(_rk, 1), 20), (2048,), 58, 12490, jnp.int32), jax.random.randint(jax.random.fold_in(jax.random.fold_in(_rk, 1), 21), (2048,), 25, 99874, jnp.int32), jax.random.randint(jax.random.fold_in(jax.random.fold_in(_rk, 1), 22), (2048,), 14, 99866, jnp.int32), jax.random.randint(jax.random.fold_in(jax.random.fold_in(_rk, 1), 23), (2048,), 97, 99829, jnp.int32), jax.random.randint(jax.random.fold_in(jax.random.fold_in(_rk, 1), 24), (2048,), 185, 99903, jnp.int32), jax.random.randint(jax.random.fold_in(jax.random.fold_in(_rk, 1), 25), (2048,), 142, 99974, jnp.int32), jax.random.randint(jax.random.fold_in(jax.random.fold_in(_rk, 1), 26), (2048,), 64, 99770, jnp.int32), jax.random.randint(jax.random.fold_in(jax.random.fold_in(_rk, 1), 27), (2048,), 32, 99905, jnp.int32), jax.random.randint(jax.random.fold_in(jax.random.fold_in(_rk, 1), 28), (2048,), 89, 12462, jnp.int32), jax.random.randint(jax.random.fold_in(jax.random.fold_in(_rk, 1), 29), (2048,), 35, 99994, jnp.int32), jax.random.randint(jax.random.fold_in(jax.random.fold_in(_rk, 1), 30), (2048,), 203, 99911, jnp.int32), jax.random.randint(jax.random.fold_in(jax.random.fold_in(_rk, 1), 31), (2048,), 3, 99940, jnp.int32), jax.random.randint(jax.random.fold_in(jax.random.fold_in(_rk, 1), 32), (2048,), 15, 99969, jnp.int32), jax.random.randint(jax.random.fold_in(jax.random.fold_in(_rk, 1), 33), (2048,), 565, 99947, jnp.int32), jax.random.randint(jax.random.fold_in(jax.random.fold_in(_rk, 1), 34), (2048,), 221, 99937, jnp.int32), jax.random.randint(jax.random.fold_in(jax.random.fold_in(_rk, 1), 35), (2048,), 48, 99687, jnp.int32), jax.random.randint(jax.random.fold_in(jax.random.fold_in(_rk, 1), 36), (2048,), 85, 99979, jnp.int32), jax.random.randint(jax.random.fold_in(jax.random.fold_in(_rk, 1), 37), (2048,), 12, 12454, jnp.int32), jax.random.randint(jax.random.fold_in(jax.random.fold_in(_rk, 1), 38), (2048,), 37, 12499, jnp.int32), jax.random.randint(jax.random.fold_in(jax.random.fold_in(_rk, 1), 39), (2048,), 113, 99917, jnp.int32), jax.random.randint(jax.random.fold_in(jax.random.fold_in(_rk, 1), 40), (2048,), 6, 12492, jnp.int32), jax.random.randint(jax.random.fold_in(jax.random.fold_in(_rk, 1), 41), (2048,), 81, 99796, jnp.int32), jax.random.randint(jax.random.fold_in(jax.random.fold_in(_rk, 1), 42), (2048,), 37, 99799, jnp.int32), jax.random.randint(jax.random.fold_in(jax.random.fold_in(_rk, 1), 43), (2048,), 18, 99979, jnp.int32), jax.random.randint(jax.random.fold_in(jax.random.fold_in(_rk, 1), 44), (2048,), 146, 99921, jnp.int32), jax.random.randint(jax.random.fold_in(jax.random.fold_in(_rk, 1), 45), (2048,), 19, 12498, jnp.int32), jax.random.randint(jax.random.fold_in(jax.random.fold_in(_rk, 1), 46), (2048,), 67, 99859, jnp.int32), jax.random.randint(jax.random.fold_in(jax.random.fold_in(_rk, 1), 47), (2048,), 88, 12486, jnp.int32), jax.random.randint(jax.random.fold_in(jax.random.fold_in(_rk, 1), 48), (2048,), 199, 99913, jnp.int32), jax.random.randint(jax.random.fold_in(jax.random.fold_in(_rk, 1), 49), (2048,), 60, 99900, jnp.int32)], axis=1)
        r_input_mask = jax.random.randint(jax.random.fold_in(_rk, 2), (2048, 50), 1, 2, jnp.int32)
        return (r_input_ids, r_input_mask)
    r_input_ids, r_input_mask = _rec_inputs()

    def _L0_rec_setup():
        import jax, jax.numpy as jnp
        import numpy as np
        V = 12500
        H = 128
        B = 1024
        T = 50

        def _gru_scan(x, kernel, rec_kernel, bias):
            b_i, b_r = (bias[0], bias[1])
            xp = jnp.einsum('bth,hk->btk', x, kernel) + b_i

            def step(h, xt):
                rec = h @ rec_kernel + b_r
                xz, xr, xh = jnp.split(xt, 3, axis=-1)
                rz, rr, rh = jnp.split(rec, 3, axis=-1)
                z = jax.nn.sigmoid(xz + rz)
                r = jax.nn.sigmoid(xr + rr)
                hh = jnp.tanh(xh + r * rh)
                h_new = z * h + (1.0 - z) * hh
                return (h_new, h_new)
            h0 = jnp.zeros((x.shape[0], rec_kernel.shape[0]), dtype=x.dtype)
            _, hs = jax.lax.scan(step, h0, jnp.swapaxes(xp, 0, 1))
            return jnp.swapaxes(hs, 0, 1)
        key = jax.random.key(seed)
        k1, k2, k3, k4 = jax.random.split(key, 4)
        input_ids = jax.random.randint(k1, (B, T), 0, V + 1, dtype=jnp.int64)
        input_mask = jnp.ones((B, T), dtype=jnp.int64)
        emb_table = jax.random.normal(k2, (V + 1, H), dtype=jnp.float32) * 0.05
        gru_kernel = jax.random.normal(k3, (H, 3 * H), dtype=jnp.float32) * 0.05
        gru_rec_kernel = jax.random.normal(k4, (H, 3 * H), dtype=jnp.float32) * 0.05
        gru_bias = jnp.zeros((2, 3 * H), dtype=jnp.float32)
        return {'input_ids': input_ids, 'input_mask': input_mask, 'emb_table': emb_table, 'gru_kernel': gru_kernel, 'gru_rec_kernel': gru_rec_kernel, 'gru_bias': gru_bias}
    _L0_rec_all = _L0_rec_setup()
    _L0_rec_in = {k: v for k, v in _L0_rec_all.items() if k in ('emb_table', 'gru_kernel', 'gru_rec_kernel', 'gru_bias')}
    del _L0_rec_all
    return {'r_input_ids': r_input_ids, 'r_input_mask': r_input_mask, 'L0_rec_emb_table': _L0_rec_in['emb_table'], 'L0_rec_gru_kernel': _L0_rec_in['gru_kernel'], 'L0_rec_gru_rec_kernel': _L0_rec_in['gru_rec_kernel'], 'L0_rec_gru_bias': _L0_rec_in['gru_bias']}

def reference(r_input_ids, r_input_mask, L0_rec_emb_table, L0_rec_gru_kernel, L0_rec_gru_rec_kernel, L0_rec_gru_bias):
    import jax
    import jax.numpy as jnp

    def _L0_rec_ref(input_ids, input_mask, emb_table, gru_kernel, gru_rec_kernel, gru_bias):
        import jax, jax.numpy as jnp
        import numpy as np
        V = 12500
        H = 128
        B = 1024
        T = 50

        def _gru_scan(x, kernel, rec_kernel, bias):
            b_i, b_r = (bias[0], bias[1])
            xp = jnp.einsum('bth,hk->btk', x, kernel) + b_i

            def step(h, xt):
                rec = h @ rec_kernel + b_r
                xz, xr, xh = jnp.split(xt, 3, axis=-1)
                rz, rr, rh = jnp.split(rec, 3, axis=-1)
                z = jax.nn.sigmoid(xz + rz)
                r = jax.nn.sigmoid(xr + rr)
                hh = jnp.tanh(xh + r * rh)
                h_new = z * h + (1.0 - z) * hh
                return (h_new, h_new)
            h0 = jnp.zeros((x.shape[0], rec_kernel.shape[0]), dtype=x.dtype)
            _, hs = jax.lax.scan(step, h0, jnp.swapaxes(xp, 0, 1))
            return jnp.swapaxes(hs, 0, 1)
        x = emb_table[input_ids]
        hs = _gru_scan(x, gru_kernel, gru_rec_kernel, gru_bias)
        lengths = jnp.sum(input_mask, axis=1).astype(jnp.int32)
        last = jnp.take_along_axis(hs, (lengths - 1)[:, None, None], axis=1)[:, 0]
        logits = last @ emb_table.T
        return logits
    y = _L0_rec_ref(r_input_ids, r_input_mask, L0_rec_emb_table, L0_rec_gru_kernel, L0_rec_gru_rec_kernel, L0_rec_gru_bias)
    return y

_drawn_inputs = setup_inputs


def setup_inputs(seed=0):
    import zlib

    import numpy as np

    out = dict(_drawn_inputs(seed))
    spreads = {'L0_rec_gru_bias': (0.0, 0.1)}
    factors = {}
    for name, (base, spread) in spreads.items():
        noise = np.random.default_rng([zlib.crc32(name.encode()), seed]).standard_normal(out[name].shape)
        drawn = base * np.exp(spread * noise) if base else spread * noise
        out[name] = jnp.asarray(drawn.astype(out[name].dtype))
    for name, factor in factors.items():
        out[name] = (out[name] * factor).astype(out[name].dtype)
    return out
```

```python
from contextlib import ExitStack

import concourse.bass as bass
from concourse import mybir

F32 = mybir.dt.float32
F32R = mybir.dt.float32r
I32 = mybir.dt.int32
U32 = mybir.dt.uint32
ALU = mybir.AluOpType
ACT = mybir.ActivationFunctionType
AX = mybir.AxisListType

P = 128
BLOCK = 512
CHUNK = 512
BIG = 1.0e30
HUGE = 3.0e38


def gru_logits(nc, ids, mask, emb, w_in, w_rec, bias, out):
    B, T = ids.shape
    V, H = emb.shape
    G = 3 * H
    NT = B // P
    HALVES = 2
    TPH = NT // HALVES
    TPB = BLOCK // P
    BPS = TPH // TPB
    SPI = 2
    QS = SPI * BPS
    ITERS = T // SPI
    BLOCKS = ITERS * QS
    UPQ = TPH // QS
    TPC = CHUNK // P
    FULL = V // CHUNK
    REST = V - FULL * CHUNK
    VP = V + V % 2
    PAIRS = FULL // 2
    WHOLE = [(j, P) for j in range(TPC)]
    RAGGED = [(j, min(P, REST - j * P)) for j in range((REST + P - 1) // P)]
    assert H == P and BPS == 2 and UPQ == 2 and T % SPI == 0 and FULL % 2 == 0
    assert ITERS == FULL + 1

    table = nc.dram_tensor("gate_table", [V + 1, G], F32).ap()
    out_v = out.rearrange("(p n) v -> p n v", n=NT)

    with ExitStack() as ctx:
        def sb(name, shape, dt=F32):
            return ctx.enter_context(nc.sbuf_tensor(name, shape, dt))

        def psum(name, shape):
            return ctx.enter_context(nc.psum_tensor(name, shape, F32))

        def sem(name):
            return ctx.enter_context(nc.semaphore(name))

        ident = sb("ident", [P, P])
        w_in_sb = sb("w_in_sb", [P, G])
        w_rec_sb = sb("w_rec_sb", [P, G])
        bias_sb = sb("bias_sb", [P, 2, 3])
        zr_bias = sb("zr_bias", [P, 2])
        warm = sb("warm", [P, BPS])
        nan_row = sb("nan_row", [P, NT])
        index = sb("index", [P, HALVES * BLOCKS, TPB], U32)
        index_now = sb("index_now", [P, QS, TPB], U32)
        gathered = sb("gathered", [P, QS, TPB, G])
        state = sb("state", [P, HALVES, BPS, BLOCK])
        state_hi = sb("state_hi", [P, TPH * P], F32R)
        state_lo = sb("state_lo", [P, TPH * P], F32R)
        z_sb = sb("z_sb", [P, BPS, BLOCK])
        r_sb = sb("r_sb", [P, BPS, BLOCK])
        cand = sb("cand", [P, BPS, BLOCK])
        kept = sb("kept", [P, BPS, BLOCK])
        emb_rows = sb("emb_rows", [P, 2, TPC, H])
        embT_hi = sb("embT_hi", [P, VP], F32R)
        embT_lo = sb("embT_lo", [P, VP], F32R)
        logits = sb("logits", [P, TPH, CHUNK])
        length = sb("length", [P, NT])
        last = sb("last", [P, NT])
        wrap = sb("wrap", [P, NT])
        bad = sb("bad", [P, NT])
        t_int = sb("t_int", [P, T], I32)
        t_f32 = sb("t_f32", [P, T])
        table_rows = gathered[:].rearrange("p q n g -> p (q n g)")[:, 0:2 * TPC * G].rearrange(
            "p (s n g) -> p s n g", s=2, g=G)
        embT_now = kept
        freeze_row = r_sb[0:1, 0, 0:G]
        scratch = logits[:].rearrange("p n v -> p (n v)")
        ids_sb = scratch[:, 0:NT * T].bitcast(I32)
        mask_sb = scratch[:, NT * T:2 * NT * T].bitcast(I32)
        row_f = scratch[:, 2 * NT * T:3 * NT * T]
        flag_f = scratch[:, 3 * NT * T:4 * NT * T]

        z_ps = psum("z_ps", [P, BPS, BLOCK])
        r_ps = psum("r_ps", [P, BPS, BLOCK])
        c_ps = psum("c_ps", [P, BPS, BLOCK])
        x_ps = psum("x_ps", [P, 2, CHUNK])

        s_ids = sem("s_ids")
        s_small = sem("s_small")
        s_zeroed = sem("s_zeroed")
        s_ident = sem("s_ident")
        s_iota = sem("s_iota")
        s_bias = sem("s_bias")
        s_math = sem("s_math")
        s_freeze_row = sem("s_freeze_row")
        s_freeze_out = sem("s_freeze_out")
        s_emb = [sem(f"s_emb{k}") for k in range(2)]
        s_embT_ps = sem("s_embT_ps")
        s_embT_now = sem("s_embT_now")
        s_proj = sem("s_proj")
        s_proj_dve = sem("s_proj_dve")
        s_proj_act = sem("s_proj_act")
        s_table = [sem(f"s_table{k}") for k in range(2)]
        s_index = [sem(f"s_index{q}") for q in range(QS)]
        s_go = sem("s_go")
        s_gather = [sem(f"s_gather{q}") for q in range(QS)]
        s_turned = sem("s_turned")
        s_rec = sem("s_rec")
        s_z_in = sem("s_z_in")
        s_r = sem("s_r")
        s_z = sem("s_z")
        s_scaled = sem("s_scaled")
        s_cand = sem("s_cand")
        s_kept = sem("s_kept")
        s_new = sem("s_new")
        s_state = sem("s_state")
        s_rows = sem("s_rows")
        s_rowsT = sem("s_rowsT")
        s_hi = sem("s_hi")
        s_lo = sem("s_lo")
        s_split = sem("s_split")
        s_unit = sem("s_unit")
        s_unit_act = sem("s_unit_act")
        s_unit_dve = sem("s_unit_dve")
        s_out = [sem(f"s_out{q}") for q in range(QS)]

        def emb_chunk(chunk):
            return emb[bass.ds(chunk * CHUNK, CHUNK), :].rearrange("(n p) h -> p n h", p=P)

        block = ctx.enter_context(nc.Block())

        @block.sync
        def _(sp):
            sp.dma_start(w_in_sb[:], w_in).then_inc(s_small, 16)
            sp.dma_start(emb_rows[:, 0], emb_chunk(0)).then_inc(s_emb[0], 16)
            sp.dma_start(emb_rows[:, 1], emb_chunk(1)).then_inc(s_emb[1], 16)
            sp.dma_start(w_rec_sb[:], w_rec).then_inc(s_small, 16)
            sp.dma_start(ids_sb, ids.rearrange("(p n) t -> p (n t)", n=NT)).then_inc(s_ids, 16)
            sp.dma_start(mask_sb, mask.rearrange("(p n) t -> p (n t)", n=NT)).then_inc(s_ids, 16)
            with nc.allow_non_contiguous_dma(reason="768 words of bias, once"):
                for k in range(2):
                    sp.dma_start(bias_sb[:, k, :], bias[k].rearrange("(g p) -> p g", p=P)).then_inc(s_small, 16)
            sp.wait_ge(s_freeze_row, 2)
            sp.dma_start(table[V:V + 1, :], freeze_row).then_inc(s_freeze_out, 16)

            def store_rows(chunk, k):
                sp.wait_ge(s_proj_dve, (chunk + 1) * (TPC // 2))
                sp.wait_ge(s_proj_act, (chunk + 1) * (TPC // 2))
                sp.dma_start(table[bass.ds(chunk * CHUNK, CHUNK), :].rearrange("(n p) g -> p n g", p=P),
                             table_rows[:, k]).then_inc(s_table[k], 16)

            with sp.Fori(0, PAIRS - 1) as i:
                for k in range(2):
                    sp.wait_ge(s_embT_ps, 2 * i + k + 1)
                    sp.dma_start(emb_rows[:, k], emb_chunk(2 * i + 2 + k)).then_inc(s_emb[k], 16)
                    store_rows(2 * i + k, k)
            sp.wait_ge(s_embT_ps, FULL - 1)
            for j, m in RAGGED:
                sp.dma_start(emb_rows[0:m, 0, j, :], emb[FULL * CHUNK + j * P:FULL * CHUNK + j * P + m, :]).then_inc(s_emb[0], 16)
            store_rows(FULL - 2, 0)
            store_rows(FULL - 1, 1)
            sp.wait_ge(s_proj_dve, FULL * (TPC // 2) + 1)
            sp.wait_ge(s_proj_act, FULL * (TPC // 2) + 1)
            for j, m in RAGGED:
                sp.dma_start(table[FULL * CHUNK + j * P:FULL * CHUNK + j * P + m, :], table_rows[0:m, 0, j, :]).then_inc(s_table[0], 16)

            def place_index(it, q, first=False):
                if not first:
                    sp.wait_ge(s_gather[q], 16 * TPB * it)
                sp.dma_start(index_now[:, q, :], index[:, bass.ds(it * QS + q, 1), :].rearrange("p a n -> p (a n)")).then_inc(s_index[q], 16)

            def put(half, it, q, v0, width):
                n = half * TPH + q * UPQ
                sp.wait_ge(s_unit_act, it * QS + q + 1)
                sp.wait_ge(s_unit_dve, it * QS + q + 1)
                sp.dma_start(out_v[:, n:n + UPQ, bass.ds(v0, width)],
                             logits[:, q * UPQ:(q + 1) * UPQ, 0:width]).then_inc(s_out[q], 16)

            sp.wait_ge(s_math, MATH_STEPS)
            for q in range(QS):
                place_index(0, q, first=True)
            sp.wait_ge(s_embT_ps, FULL + 1)
            for j, m in RAGGED:
                sp.dma_start(emb_rows[0:m, 0, j, :], emb[FULL * CHUNK + j * P:FULL * CHUNK + j * P + m, :]).then_inc(s_rows, 16)
            for q in range(QS):
                place_index(1, q)
            with sp.Fori(1, ITERS) as i:
                sp.wait_ge(s_rowsT, i)
                sp.dma_start(emb_rows[:, 0], emb_chunk(i - 1)).then_inc(s_rows, 16)
                for q in range(QS):
                    place_index(i + 1, q)
            for q in range(QS):
                place_index(ITERS + 1, q)
                put(0, 0, q, FULL * CHUNK, REST)
            with sp.Fori(1, ITERS - 1) as i:
                for q in range(QS):
                    place_index(i + (ITERS + 1), q)
                    put(0, i, q, (i - 1) * CHUNK, CHUNK)
            for q in range(QS):
                put(0, ITERS - 1, q, (FULL - 1) * CHUNK, CHUNK)
            for q in range(QS):
                put(1, ITERS, q, FULL * CHUNK, REST)
            with sp.Fori(1, ITERS) as i:
                for q in range(QS):
                    put(1, i + ITERS, q, (i - 1) * CHUNK, CHUNK)
            for q in range(QS):
                sp.wait_ge(s_out[q], 16 * HALVES * ITERS)

        @block.gpsimd
        def _(pool):
            nc.gpsimd.memset(ident[:], 0.0).then_inc(s_zeroed, 1)
            nc.gpsimd.iota(t_int[:], pattern=[[1, T]], base=0, channel_multiplier=0).then_inc(s_iota, 1)
            pool.wait_ge(s_zeroed, 1)
            nc.gpsimd.affine_select(out=ident[:], in_=ident[:], compare_op=ALU.not_equal, fill=1.0, base=0,
                                    pattern=[[-1, P]], channel_multiplier=1).then_inc(s_ident, 1)
            pool.wait_ge(s_table[0], 16 * (PAIRS + len(RAGGED)))
            pool.wait_ge(s_table[1], 16 * PAIRS)
            pool.wait_ge(s_freeze_out, 16)

            def gather(it, q, first=False):
                if not first:
                    pool.wait_ge(s_turned, (it - 1) * QS + q + 1)
                pool.wait_ge(s_index[q], 16 * (it + 1))
                pool.sem_inc(s_go, 1)
                for n in range(TPB):
                    nc.gpsimd.indirect_dma_start(
                        gathered[:, q, n, :], None, table,
                        bass.IndirectOffsetOnAxis(ap=index_now[:, q, n:n + 1], axis=0)).then_inc(s_gather[q], 16)

            for q in range(QS):
                gather(0, q, first=True)
            with pool.Fori(1, HALVES * ITERS) as i:
                for q in range(QS):
                    gather(i, q)

        @block.tensor
        def _(pe):
            pe.wait_ge(s_ident, 1)
            pe.wait_ge(s_small, 16 * 4)

            def transpose_rows(c, k, landed, tiles=WHOLE, first=False):
                pe.wait_ge(s_emb[k], 16 * landed)
                if not first:
                    pe.wait_ge(s_embT_now, c - 1)
                for j, m in tiles:
                    turned = nc.tensor.transpose(x_ps[:, k, j * P:j * P + m], emb_rows[0:m, k, j, :], ident[0:m, 0:m])
                turned.then_inc(s_embT_ps, 1)

            def project(c, k, tiles=WHOLE, first=False):
                pe.wait_ge(s_embT_now, c + 1)
                for j, m in tiles:
                    if not (first and j < 4):
                        pe.wait_ge((s_proj_dve, s_proj_act)[j % 2], c * (TPC // 2) + j // 2 - 1)
                    bank = (z_ps, r_ps)[j // 2]
                    nc.tensor.matmul(bank[0:m, j % 2, 0:G], embT_now[:, k, j * P:j * P + m], w_in_sb[:],
                                     start=True, stop=True).then_inc(s_proj, 1)

            transpose_rows(0, 0, 1, first=True)
            transpose_rows(1, 1, 1, first=True)
            project(0, 0, first=True)
            transpose_rows(2, 0, 2)
            project(1, 1)
            with pe.Fori(1, PAIRS - 1) as i:
                for k in range(2):
                    transpose_rows(2 * i + k + 1, 1 - k, i + 1 + k)
                    project(2 * i + k, k)
            transpose_rows(FULL - 1, 1, PAIRS)
            project(FULL - 2, 0)
            transpose_rows(FULL, 0, PAIRS + len(RAGGED), tiles=RAGGED)
            project(FULL - 1, 1)
            project(FULL, 0, tiles=RAGGED)

            def add_rows(bank, q, gate, first):
                for n in range(TPB):
                    turned = nc.tensor.matmul(bank[:, n * P:(n + 1) * P], gathered[:, q, n, gate * H:(gate + 1) * H],
                                              ident[:], is_transpose=True, start=(first and n == 0), stop=True,
                                              skip_group_check=True)
                return turned

            def add_rec(bank, h, gate, first):
                return nc.tensor.matmul(bank, w_rec_sb[:, gate * H:(gate + 1) * H], h, start=first, stop=True,
                                        skip_group_check=True)

            def step(half, it, q, before=None, after=None):
                g = it * QS + q
                b = q % BPS
                h = state[:, half, b, :]
                pe.wait_ge(s_gather[q], 16 * TPB * (it + 1))
                pe.wait_ge(s_z, g + 1)
                add_rows(r_ps[:, b], q, 1, True)
                pe.wait_ge(s_state, g + 1)
                add_rec(r_ps[:, b], h, 1, False).then_inc(s_rec, 1)
                add_rec(c_ps[:, b], h, 2, True).then_inc(s_rec, 1)
                add_rows(z_ps[:, b], q, 0, True)
                add_rec(z_ps[:, b], h, 0, False).then_inc(s_z_in, 1)
                if before is not None:
                    before()
                pe.wait_ge(s_scaled, g + 1)
                add_rows(c_ps[:, b], q, 2, False).then_inc(s_turned, 1)
                if after is not None:
                    after()

            def vocabulary(landed, copied, tiles):
                def work():
                    pe.wait_ge(s_rows, landed)
                    if copied is not None:
                        pe.wait_ge(s_lo, copied)
                    for j, m in tiles:
                        turned = nc.tensor.transpose(x_ps[:, 0, j * P:j * P + m], emb_rows[0:m, 0, j, :], ident[0:m, 0:m])
                    turned.then_inc(s_rowsT, 1)
                return work

            def unit(it, q, j, v0, width, ready=None):
                def work():
                    if ready is not None:
                        pe.wait_ge(s_split, ready)
                    if ready is None or it:
                        pe.wait_ge((s_unit_act, s_unit_dve)[j], it * QS + q)
                    elif q:
                        pe.wait_ge((s_unit_act, s_unit_dve)[j], q)
                    else:
                        pe.wait_ge(s_lo, ITERS)
                    n = q * UPQ + j
                    even = width + width % 2
                    for part, (h, e) in enumerate(((state_hi, embT_hi), (state_hi, embT_lo), (state_lo, embT_hi))):
                        product = nc.tensor.matmul(x_ps[:, j, 0:even], h[:, n * P:(n + 1) * P], e[:, bass.ds(v0, even)],
                                                   start=(part == 0), stop=(part == 2))
                    product.then_inc(s_unit, 1)
                return work

            for q in range(QS):
                step(0, 0, q, before=vocabulary(16 * len(RAGGED), None, RAGGED) if q == 0 else None)
            with pe.Fori(1, ITERS) as i:
                for q in range(QS):
                    step(0, i, q, before=vocabulary(16 * i + 16 * len(RAGGED), i, WHOLE) if q == 0 else None)
            for q in range(QS):
                step(1, ITERS, q, *[unit(0, q, j, FULL * CHUNK, REST, ready=2) for j in range(UPQ)])
            with pe.Fori(1, ITERS) as i:
                for q in range(QS):
                    step(1, i + ITERS, q, *[unit(i, q, j, (i - 1) * CHUNK, CHUNK) for j in range(UPQ)])
            for q in range(QS):
                for j in range(UPQ):
                    unit(ITERS, q, j, FULL * CHUNK, REST, ready=4)()
            with pe.Fori(1, ITERS) as i:
                for q in range(QS):
                    for j in range(UPQ):
                        unit(i + ITERS, q, j, (i - 1) * CHUNK, CHUNK)()

        @block.scalar
        def _(act):
            act.wait_ge(s_bias, 1)
            for b in range(BPS):
                nc.scalar.activation(warm[:, b:b + 1], zr_bias[:, b:b + 1], ACT.Sigmoid).then_inc(s_z, 1)

            def table_chunk(c, k, stored, tiles=TPC, width=CHUNK):
                act.wait_ge(s_embT_ps, c + 1)
                if stored is not None:
                    act.wait_ge(s_proj, (c - 1) * TPC)
                nc.scalar.copy(embT_now[:, k, 0:width], x_ps[:, k, 0:width]).then_inc(s_embT_now, 1)
                for j in range(1, tiles, 2):
                    act.wait_ge(s_proj, c * TPC + j + 1)
                    if stored is not None and j == 1:
                        act.wait_ge(s_table[k], 16 * stored)
                    m = min(P, width - j * P)
                    nc.scalar.copy(table_rows[0:m, k, j, :], (z_ps, r_ps)[j // 2][0:m, 1, 0:G]).then_inc(s_proj_act, 1)

            for k in range(2):
                table_chunk(k, k, None)
            with act.Fori(1, PAIRS) as i:
                for k in range(2):
                    table_chunk(2 * i + k, k, i)
            table_chunk(FULL, 0, PAIRS, tiles=len(RAGGED), width=REST)

            def gates(it, q, meanwhile=None, after=None):
                g = it * QS + q
                b = q % BPS
                act.wait_ge(s_rec, 2 * g + 1)
                nc.scalar.activation(r_sb[:, b], r_ps[:, b], ACT.Sigmoid, bias=zr_bias[:, 1:2]).then_inc(s_r, 1)
                act.wait_ge(s_z_in, g + 1)
                nc.scalar.activation(z_sb[:, b], z_ps[:, b], ACT.Sigmoid, bias=zr_bias[:, 0:1]).then_inc(s_z, 1)
                if meanwhile is not None:
                    meanwhile()
                act.wait_ge(s_turned, g + 1)
                nc.scalar.activation(cand[:, b], c_ps[:, b], ACT.Tanh, bias=bias_sb[:, 0, 2:3]).then_inc(s_cand, 1)
                if after is not None:
                    after()

            def high_part(n, v0, width):
                def work():
                    act.wait_ge(s_rowsT, n)
                    nc.scalar.copy(embT_hi[:, bass.ds(v0, width)], x_ps[:, 0, 0:width]).then_inc(s_hi, 1)
                return work

            def copy_unit(half, it, q, width, first=False):
                def work():
                    n = q * UPQ
                    act.wait_ge(s_unit, it * TPH + n + 1)
                    if not first:
                        act.wait_ge(s_out[q], 16 * it)
                    nc.scalar.activation(logits[:, n, 0:width], x_ps[:, 0, 0:width], ACT.Identity,
                                         bias=nan_row[:, half * TPH + n:half * TPH + n + 1]).then_inc(s_unit_act, 1)
                return work

            for q in range(QS):
                gates(0, q, high_part(1, FULL * CHUNK, REST) if q == 0 else None)
            with act.Fori(1, ITERS) as i:
                for q in range(QS):
                    gates(i, q, high_part(i + 1, (i - 1) * CHUNK, CHUNK) if q == 0 else None)
            for q in range(QS):
                gates(ITERS, q, after=copy_unit(0, 0, q, REST, first=True))
            with act.Fori(1, ITERS) as i:
                for q in range(QS):
                    gates(i + ITERS, q, after=copy_unit(0, i, q, CHUNK))
            for q in range(QS):
                copy_unit(1, ITERS, q, REST)()
            with act.Fori(1, ITERS) as i:
                for q in range(QS):
                    copy_unit(1, i + ITERS, q, CHUNK)()

        @block.vector
        def _(dve):
            nc.vector.memset(freeze_row[:, 0:H], BIG).then_inc(s_freeze_row, 1)
            nc.vector.memset(freeze_row[:, H:G], 0.0).then_inc(s_freeze_row, 1)
            for b in range(BPS):
                nc.vector.memset(state[:, :, b, :], 0.0).then_inc(s_state, 1)
            if VP > V:
                nc.vector.memset(embT_hi[:, V:VP].bitcast(F32), 0.0)
                nc.vector.memset(embT_lo[:, V:VP].bitcast(F32), 0.0)
            dve.wait_ge(s_small, 16 * 4)
            nc.vector.tensor_tensor(zr_bias[:], bias_sb[:, 0, 0:2], bias_sb[:, 1, 0:2], ALU.add).then_inc(s_bias, 1)

            def table_chunk(c, k, stored, tiles=TPC, width=CHUNK):
                for j in range(0, tiles, 2):
                    dve.wait_ge(s_proj, c * TPC + j + 1)
                    if stored is not None and j == 0:
                        dve.wait_ge(s_table[k], 16 * stored)
                    m = min(P, width - j * P)
                    nc.vector.tensor_copy(table_rows[0:m, k, j, :], (z_ps, r_ps)[j // 2][0:m, 0, 0:G]).then_inc(s_proj_dve, 1)

            def indices():
                steps = [0]

                def chained(ins):
                    steps[0] += 1
                    ins.then_inc(s_math, 1)
                    dve.wait_ge(s_math, steps[0])

                dve.wait_ge(s_ids, 32)
                dve.wait_ge(s_iota, 1)
                chained(nc.vector.tensor_reduce(length[:], mask_sb.rearrange("p (n t) -> p n t", t=T), AX.X, ALU.add))
                chained(nc.vector.tensor_scalar(length[:], length[:], -1.0, None, ALU.add))
                chained(nc.vector.tensor_scalar(wrap[:], length[:], 0.0, float(T), ALU.is_lt, ALU.mult))
                chained(nc.vector.tensor_tensor(last[:], length[:], wrap[:], ALU.add))
                chained(nc.vector.tensor_scalar(bad[:], last[:], 0.0, None, ALU.is_lt))
                chained(nc.vector.tensor_scalar(wrap[:], last[:], float(T - 1), None, ALU.is_gt))
                chained(nc.vector.tensor_tensor(bad[:], bad[:], wrap[:], ALU.add))
                chained(nc.vector.tensor_scalar(bad[:], bad[:], HUGE, HUGE, ALU.mult, ALU.mult))
                chained(nc.vector.tensor_tensor(nan_row[:], bad[:], bad[:], ALU.subtract))
                chained(nc.vector.tensor_copy(row_f, ids_sb))
                chained(nc.vector.tensor_scalar(flag_f, row_f, 0.0, float(V), ALU.is_lt, ALU.mult))
                chained(nc.vector.tensor_tensor(row_f, row_f, flag_f, ALU.add))
                chained(nc.vector.tensor_scalar(row_f, row_f, 0.0, float(V - 1), ALU.max, ALU.min))
                chained(nc.vector.tensor_copy(t_f32[:], t_int[:]))
                chained(nc.vector.tensor_tensor(flag_f.rearrange("p (n t) -> p n t", t=T),
                                                t_f32[:].rearrange("p (a t) -> p a t", a=1).to_broadcast([P, NT, T]),
                                                last[:].rearrange("p (n a) -> p n a", a=1).to_broadcast([P, NT, T]), ALU.is_gt))
                for half in range(HALVES):
                    for b in range(BPS):
                        n0 = half * TPH + b * TPB
                        tokens = slice(n0 * T, (n0 + TPB) * T)
                        rows = index[:, half * BLOCKS:(half + 1) * BLOCKS, :].rearrange("p (t b) n -> p b n t", b=BPS)[:, b]
                        chained(nc.vector.scalar_tensor_tensor(
                            out=rows, in0=flag_f[:, tokens].rearrange("p (n t) -> p n t", t=T), scalar=float(V),
                            in1=row_f[:, tokens].rearrange("p (n t) -> p n t", t=T), op0=ALU.mult, op1=ALU.max))
                assert steps[0] == MATH_STEPS

            for k in range(2):
                table_chunk(k, k, None)
            indices()
            with dve.Fori(1, PAIRS) as i:
                for k in range(2):
                    table_chunk(2 * i + k, k, i)
            table_chunk(FULL, 0, PAIRS, tiles=len(RAGGED), width=REST)

            def update(half, it, q, meanwhile=None, after=None):
                g = it * QS + q
                b = q % BPS
                h = state[:, half, b, :]
                dve.wait_ge(s_rec, 2 * g + 2)
                dve.wait_ge(s_r, g + 1)
                nc.vector.scalar_tensor_tensor(out=c_ps[:, b], in0=c_ps[:, b], scalar=bias_sb[:, 1, 2:3],
                                               in1=r_sb[:, b], op0=ALU.add, op1=ALU.mult).then_inc(s_scaled, 1)
                dve.wait_ge(s_z, g + 1 + BPS)
                nc.vector.tensor_tensor(kept[:, b], z_sb[:, b], h, ALU.mult).then_inc(s_kept, 1)
                if meanwhile is not None:
                    meanwhile()
                dve.wait_ge(s_cand, g + 1)
                nc.vector.scalar_tensor_tensor(out=cand[:, b], in0=z_sb[:, b], scalar=-1.0, in1=cand[:, b],
                                               op0=ALU.add, op1=ALU.mult).then_inc(s_new, 1)
                dve.wait_ge(s_kept, g + 1)
                dve.wait_ge(s_new, g + 1)
                nc.vector.tensor_tensor(h, kept[:, b], cand[:, b], ALU.subtract).then_inc(s_state, 1)
                if after is not None:
                    after()

            def low_part(n, v0, width):
                def work():
                    dve.wait_ge(s_hi, n)
                    nc.vector.tensor_tensor(embT_lo[:, bass.ds(v0, width)], x_ps[:, 0, 0:width],
                                            embT_hi[:, bass.ds(v0, width)].bitcast(F32), ALU.subtract).then_inc(s_lo, 1)
                return work

            def split_state(half):
                h = state[:, half].rearrange("p b c -> p (b c)")
                dve.wait_ge(s_state, BPS + (half + 1) * BLOCKS)
                nc.vector.tensor_copy(state_hi[:], h).then_inc(s_split, 1)
                dve.wait_ge(s_split, 2 * half + 1)
                nc.vector.tensor_tensor(state_lo[:], h, state_hi[:].bitcast(F32), ALU.subtract).then_inc(s_split, 1)

            def copy_unit(half, it, q, width, first=False):
                def work():
                    n = q * UPQ + 1
                    dve.wait_ge(s_unit, it * TPH + n + 1)
                    if not first:
                        dve.wait_ge(s_out[q], 16 * it)
                    nc.vector.tensor_scalar(logits[:, n, 0:width], x_ps[:, 1, 0:width],
                                            nan_row[:, half * TPH + n:half * TPH + n + 1], None,
                                            ALU.add).then_inc(s_unit_dve, 1)
                return work

            for q in range(QS):
                update(0, 0, q, low_part(1, FULL * CHUNK, REST) if q == 0 else None)
            with dve.Fori(1, ITERS) as i:
                for q in range(QS):
                    update(0, i, q, low_part(i + 1, (i - 1) * CHUNK, CHUNK) if q == 0 else None)
            split_state(0)
            for q in range(QS):
                update(1, ITERS, q, after=copy_unit(0, 0, q, REST, first=True))
            with dve.Fori(1, ITERS) as i:
                for q in range(QS):
                    update(1, i + ITERS, q, after=copy_unit(0, i, q, CHUNK))
            split_state(1)
            for q in range(QS):
                copy_unit(1, ITERS, q, REST)()
            with dve.Fori(1, ITERS) as i:
                for q in range(QS):
                    copy_unit(1, i + ITERS, q, CHUNK)()


MATH_STEPS = 19

_INS = ['r_input_ids', 'r_input_mask', 'L0_rec_emb_table', 'L0_rec_gru_kernel', 'L0_rec_gru_rec_kernel',
        'L0_rec_gru_bias']


def kernel(**inputs):
    import numpy as _np
    import concourse.bacc as _bacc
    from concourse import mybir as _mybir
    from concourse.bass_utils import run_bass_kernel_spmd as _run

    nc = _bacc.Bacc("TRN2", target_bir_lowering=False, num_devices=1)
    arrays, args = {}, []
    for name in _INS:
        a = _np.ascontiguousarray(inputs[name])
        arrays[f"in_{name}_dram"] = a
        args.append(nc.dram_tensor(f"in_{name}_dram", a.shape, _mybir.dt.from_np(a.dtype), kind="ExternalInput").ap())
    shape = (inputs['r_input_ids'].shape[0], inputs['L0_rec_emb_table'].shape[0])
    args.append(nc.dram_tensor("out_0_dram", shape, F32, kind="ExternalOutput").ap())
    gru_logits(nc, *args)
    r = _run(nc, [arrays], core_ids=[0])
    return r.results[0]["out_0_dram"]
```

```python
from contextlib import ExitStack

import concourse.bass as bass
from concourse import mybir

F32 = mybir.dt.float32
F32R = mybir.dt.float32r
I32 = mybir.dt.int32
U32 = mybir.dt.uint32
ALU = mybir.AluOpType
ACT = mybir.ActivationFunctionType
AX = mybir.AxisListType

P = 128
GROUP = 1024
BLOCK = GROUP // 2
BANK = 512
CHUNK = 512
BIG = 1.0e30
HUGE = 3.0e38


def gru_logits(nc, ids, mask, emb, w_in, w_rec, bias, out):
    B, T = ids.shape
    V, H = emb.shape
    G = 3 * H
    NT = B // P
    GROUPS = B // GROUP
    TPG = GROUP // P
    TPB = BLOCK // P
    BPS = GROUP // BLOCK
    SPI = 2
    QS = SPI * BPS
    ITERS = T // SPI
    BLOCKS = ITERS * QS
    UPQ = TPG // QS
    KEEP = min(3, GROUPS)
    TPC = CHUNK // P
    FULL = V // CHUNK
    REST = V - FULL * CHUNK
    VP = V + V % 2
    SLOTS = 4
    ROUNDS = FULL // SLOTS
    WHOLE = [(j, P) for j in range(TPC)]
    RAGGED = [(j, min(P, REST - j * P)) for j in range((REST + P - 1) // P)]
    assert H == P and BPS == 2 and UPQ >= 1 and T % SPI == 0 and FULL % SLOTS == 0
    assert ITERS == FULL + 1

    table = nc.dram_tensor("gate_table", [V + 1, G], F32).ap()
    out_v = out.rearrange("(p n) v -> p n v", n=NT)

    with ExitStack() as ctx:
        def sb(name, shape, dt=F32):
            return ctx.enter_context(nc.sbuf_tensor(name, shape, dt))

        def psum(name, shape):
            return ctx.enter_context(nc.psum_tensor(name, shape, F32))

        def sem(name):
            return ctx.enter_context(nc.semaphore(name))

        ident = sb("ident", [P, P], F32R)
        w_in_sb = sb("w_in_sb", [P, G])
        w_rec_sb = sb("w_rec_sb", [P, G])
        w_rec_hi = sb("w_rec_hi", [P, G], F32R)
        w_rec_lo = sb("w_rec_lo", [P, G], F32R)
        bias_sb = sb("bias_sb", [P, 2, 3])
        zr_bias = sb("zr_bias", [P, 2])
        warm = sb("warm", [P, BPS])
        nan_row = sb("nan_row", [P, NT])
        index = sb("index", [P, GROUPS * BLOCKS, TPB], U32)
        index_now = sb("index_now", [P, QS, TPB], U32)
        gathered = sb("gathered", [P, QS, TPB, G], F32R)
        state = sb("state", [P, KEEP, BPS, BLOCK])
        state_hi = sb("state_hi", [P, KEEP, BPS, BLOCK], F32R)
        state_lo = sb("state_lo", [P, KEEP, BPS, BLOCK], F32R)
        z_sb = sb("z_sb", [P, BPS, BLOCK])
        r_sb = sb("r_sb", [P, BPS, BLOCK])
        cand = sb("cand", [P, BPS, BLOCK])
        kept = sb("kept", [P, BPS, BLOCK])
        emb_rows = sb("emb_rows", [P, SLOTS, TPC, H])
        embT_hi = sb("embT_hi", [P, VP], F32R)
        embT_lo = sb("embT_lo", [P, VP], F32R)
        logits = sb("logits", [P, 8, CHUNK])
        table_rows = sb("table_rows", [P, 2, TPC, G])
        length = sb("length", [P, NT])
        last = sb("last", [P, NT])
        wrap = sb("wrap", [P, NT])
        bad = sb("bad", [P, NT])
        embT_now = kept
        freeze_row = r_sb[:].rearrange("p b c -> p (b c)")[0:1, 0:G]
        scratch = logits[:].rearrange("p n v -> p (n v)")
        ids_sb = scratch[:, 0:NT * T].bitcast(I32)
        mask_sb = scratch[:, NT * T:2 * NT * T].bitcast(I32)
        row_f = scratch[:, 2 * NT * T:3 * NT * T]
        flag_f = scratch[:, 3 * NT * T:4 * NT * T]
        t_int = scratch[:, 4 * NT * T:(4 * NT + 1) * T].bitcast(I32)
        t_f32 = scratch[:, (4 * NT + 1) * T:(4 * NT + 2) * T]

        z_ps = psum("z_ps", [P, BPS, BANK])
        r_ps = psum("r_ps", [P, BPS, BANK])
        c_ps = psum("c_ps", [P, BPS, BANK])
        x_ps = psum("x_ps", [P, 2, CHUNK])

        s_ids = sem("s_ids")
        s_small = sem("s_small")
        s_zeroed = sem("s_zeroed")
        s_ident = sem("s_ident")
        s_iota = sem("s_iota")
        s_bias = sem("s_bias")
        s_w_hi = sem("s_w_hi")
        s_w_lo = sem("s_w_lo")
        s_math = sem("s_math")
        s_freeze_row = sem("s_freeze_row")
        s_freeze_out = sem("s_freeze_out")
        s_emb = [sem(f"s_emb{s}") for s in range(SLOTS)]
        s_embT_ps = sem("s_embT_ps")
        s_embT_now = sem("s_embT_now")
        s_proj = sem("s_proj")
        s_proj_dve = sem("s_proj_dve")
        s_proj_act = sem("s_proj_act")
        s_table = [sem(f"s_table{k}") for k in range(2)]
        s_index = [sem(f"s_index{q}") for q in range(QS)]
        s_go = sem("s_go")
        s_gather = [sem(f"s_gather{q}") for q in range(QS)]
        s_turned = sem("s_turned")
        s_rec = sem("s_rec")
        s_z_in = sem("s_z_in")
        s_r = sem("s_r")
        s_z = sem("s_z")
        s_scaled = sem("s_scaled")
        s_cand = sem("s_cand")
        s_kept = sem("s_kept")
        s_new = sem("s_new")
        s_start = sem("s_start")
        s_state = sem("s_state")
        s_state_hi = sem("s_state_hi")
        s_state_lo = sem("s_state_lo")
        s_rows = sem("s_rows")
        s_rowsT = sem("s_rowsT")
        s_hi = sem("s_hi")
        s_lo = sem("s_lo")
        s_unit = sem("s_unit")
        s_copied = [sem(f"s_copied{b}") for b in range(2)]
        s_out = [sem(f"s_out{q}") for q in range(QS)]
        s_last = [sem(f"s_last{n}") for n in range(8)]

        def emb_chunk(chunk):
            return emb[bass.ds(chunk * CHUNK, CHUNK), :].rearrange("(n p) h -> p n h", p=P)

        def ragged_rows(j, m):
            return slice(FULL * CHUNK + j * P, FULL * CHUNK + j * P + m)

        block = ctx.enter_context(nc.Block())

        @block.sync
        def _(sp):
            for s in range(SLOTS):
                sp.dma_start(emb_rows[:, s], emb_chunk(s)).then_inc(s_emb[s], 16)
                if s == 0:
                    sp.dma_start(w_in_sb[:], w_in).then_inc(s_small, 16)
            sp.dma_start(w_rec_sb[:], w_rec).then_inc(s_small, 16)
            with nc.allow_non_contiguous_dma(reason="768 words of bias, once"):
                for k in range(2):
                    sp.dma_start(bias_sb[:, k, :], bias[k].rearrange("(g p) -> p g", p=P)).then_inc(s_small, 16)
            sp.dma_start(ids_sb, ids.rearrange("(p n) t -> p (n t)", n=NT)).then_inc(s_ids, 16)
            sp.dma_start(mask_sb, mask.rearrange("(p n) t -> p (n t)", n=NT)).then_inc(s_ids, 16)
            sp.wait_ge(s_freeze_row, 2)
            sp.dma_start(table[V:V + 1, :], freeze_row).then_inc(s_freeze_out, 16)

            def store_rows(chunk, k):
                sp.wait_ge(s_proj_dve, (chunk + 1) * (TPC // 2))
                sp.wait_ge(s_proj_act, (chunk + 1) * (TPC // 2))
                sp.dma_start(table[bass.ds(chunk * CHUNK, CHUNK), :].rearrange("(n p) g -> p n g", p=P),
                             table_rows[:, k]).then_inc(s_table[k], 16)

            with sp.Fori(0, ROUNDS - 1) as i:
                for s in range(SLOTS):
                    sp.wait_ge(s_embT_ps, SLOTS * i + s + 1)
                    sp.dma_start(emb_rows[:, s], emb_chunk(SLOTS * i + (SLOTS + s))).then_inc(s_emb[s], 16)
                    store_rows(SLOTS * i + s, s % 2)
            sp.wait_ge(s_embT_ps, FULL - SLOTS + 1)
            for j, m in RAGGED:
                sp.dma_start(emb_rows[0:m, 0, j, :], emb[ragged_rows(j, m), :]).then_inc(s_emb[0], 16)
            for s in range(SLOTS):
                store_rows(FULL - SLOTS + s, s % 2)
            sp.wait_ge(s_proj_dve, FULL * (TPC // 2) + 1)
            sp.wait_ge(s_proj_act, FULL * (TPC // 2) + 1)
            for j, m in RAGGED:
                sp.dma_start(table[ragged_rows(j, m), :], table_rows[0:m, 0, j, :]).then_inc(s_table[0], 16)

            def place_index(it, q, first=False):
                if not first:
                    sp.wait_ge(s_gather[q], 16 * TPB * it)
                sp.dma_start(index_now[:, q, :], index[:, bass.ds(it * QS + q, 1), :].rearrange("p a n -> p (a n)")).then_inc(s_index[q], 16)

            def put(group, it, q, v0, width):
                n = group * TPG + q * UPQ
                for j in range(UPQ):
                    u = q * UPQ + j
                    sp.wait_ge(s_copied[u % 2], it * (TPG // 2) + u // 2 + 1)
                sp.dma_start(out_v[:, n:n + UPQ, bass.ds(v0, width)],
                             logits[:, q * UPQ:(q + 1) * UPQ, 0:width]).then_inc(s_out[q], 16)

            sp.wait_ge(s_math, MATH_STEPS)
            for q in range(QS):
                place_index(0, q, first=True)
            sp.wait_ge(s_embT_ps, FULL + 1)
            for j, m in RAGGED:
                sp.dma_start(emb_rows[0:m, 0, j, :], emb[ragged_rows(j, m), :]).then_inc(s_rows, 16)
            for q in range(QS):
                place_index(1, q)
            with sp.Fori(1, ITERS) as i:
                sp.wait_ge(s_rowsT, i)
                sp.dma_start(emb_rows[:, 0], emb_chunk(i - 1)).then_inc(s_rows, 16)
                for q in range(QS):
                    place_index(i + 1, q)
            for group in range(1, GROUPS):
                it0 = group * ITERS
                made = (group - 1) * ITERS
                for q in range(QS):
                    place_index(it0 + 1, q)
                    put(group - 1, made, q, FULL * CHUNK, REST)
                with sp.Fori(1, ITERS - 1) as i:
                    for q in range(QS):
                        place_index(i + (it0 + 1), q)
                        put(group - 1, i + made, q, (i - 1) * CHUNK, CHUNK)
                for q in range(QS):
                    if group + 1 < GROUPS:
                        place_index(it0 + ITERS, q)
                    put(group - 1, made + ITERS - 1, q, (FULL - 1) * CHUNK, CHUNK)
            made = (GROUPS - 1) * ITERS

            def put_last(it, u, buffer, v0, width):
                n = (GROUPS - 1) * TPG + u
                sp.wait_ge(s_copied[u % 2], it * (TPG // 2) + u // 2 + 1)
                sp.dma_start(out_v[:, n:n + 1, bass.ds(v0, width)], logits[:, buffer:buffer + 1, 0:width]).then_inc(s_last[buffer], 16)

            for u in range(TPG):
                put_last(made, u, u, FULL * CHUNK, REST)
            with sp.Fori(0, FULL // LAST_CHUNKS) as i:
                for c in range(LAST_CHUNKS):
                    for u in range(TPG):
                        put_last(LAST_CHUNKS * i + (made + 1 + c), u, c * TPG + u, (LAST_CHUNKS * i + c) * CHUNK, CHUNK)
            for q in range(QS):
                sp.wait_ge(s_out[q], 16 * (GROUPS - 1) * ITERS)
            for n in range(8):
                sp.wait_ge(s_last[n], 16 * (FULL // LAST_CHUNKS + (n < TPG)))

        @block.gpsimd
        def _(pool):
            nc.gpsimd.memset(ident[:].bitcast(F32), 0.0).then_inc(s_zeroed, 1)
            nc.gpsimd.iota(t_int, pattern=[[1, T]], base=0, channel_multiplier=0).then_inc(s_iota, 1)
            pool.wait_ge(s_zeroed, 1)
            nc.gpsimd.affine_select(out=ident[:], in_=ident[:].bitcast(F32), compare_op=ALU.not_equal, fill=1.0, base=0,
                                    pattern=[[-1, P]], channel_multiplier=1).then_inc(s_ident, 1)
            pool.wait_ge(s_table[0], 16 * (FULL // 2 + len(RAGGED)))
            pool.wait_ge(s_table[1], 16 * (FULL // 2))
            pool.wait_ge(s_freeze_out, 16)

            def gather(it, q, first=False):
                if not first:
                    pool.wait_ge(s_turned, (it - 1) * QS + q + 1)
                pool.wait_ge(s_index[q], 16 * (it + 1))
                pool.sem_inc(s_go, 1)
                for n in range(TPB):
                    nc.gpsimd.indirect_dma_start(
                        gathered[:, q, n, :].bitcast(F32), None, table,
                        bass.IndirectOffsetOnAxis(ap=index_now[:, q, n:n + 1], axis=0)).then_inc(s_gather[q], 16)

            for q in range(QS):
                gather(0, q, first=True)
            with pool.Fori(1, GROUPS * ITERS) as i:
                for q in range(QS):
                    gather(i, q)

        @block.tensor
        def _(pe):
            ident_f = ident[:].bitcast(F32)
            pe.wait_ge(s_ident, 1)

            def transpose_rows(c, s, landed, tiles=WHOLE, first=False):
                pe.wait_ge(s_emb[s], 16 * landed)
                if not first:
                    pe.wait_ge(s_embT_now, c - 1)
                for j, m in tiles:
                    turned = nc.tensor.transpose(x_ps[:, s % 2, j * P:j * P + m], emb_rows[0:m, s, j, :], ident_f[0:m, 0:m])
                turned.then_inc(s_embT_ps, 1)

            def project(c, k, tiles=WHOLE, first=False):
                pe.wait_ge(s_embT_now, c + 1)
                for j, m in tiles:
                    if not first:
                        pe.wait_ge((s_proj_dve, s_proj_act)[j % 2], c * (TPC // 2) + j // 2 - 1)
                    bank = (z_ps, r_ps)[j // 2]
                    nc.tensor.matmul(bank[0:m, j % 2, 0:G], embT_now[:, k, j * P:j * P + m], w_in_sb[:],
                                     start=True, stop=True).then_inc(s_proj, 1)

            transpose_rows(0, 0, 1, first=True)
            transpose_rows(1, 1, 1, first=True)
            pe.wait_ge(s_small, 16 * 4)
            project(0, 0, first=True)
            for s in range(1, SLOTS):
                transpose_rows(s + 1, (s + 1) % SLOTS, 1 + (s + 1) // SLOTS)
                project(s, s % 2)
            with pe.Fori(1, ROUNDS - 1) as i:
                for s in range(SLOTS):
                    transpose_rows(SLOTS * i + (s + 1), (s + 1) % SLOTS, i + (1 + (s + 1) // SLOTS))
                    project(SLOTS * i + s, s % 2)
            for s in range(SLOTS - 1):
                transpose_rows(FULL - SLOTS + s + 1, s + 1, ROUNDS)
                project(FULL - SLOTS + s, s % 2)
            transpose_rows(FULL, 0, ROUNDS + len(RAGGED), tiles=RAGGED)
            project(FULL - 1, 1)
            project(FULL, 0, tiles=RAGGED)

            pe.wait_ge(s_w_lo, 1)

            def add_rows(bank, q, gate, first):
                for n in range(TPB):
                    turned = nc.tensor.matmul(bank[:, n * P:(n + 1) * P].bitcast(F32R), gathered[:, q, n, gate * H:(gate + 1) * H],
                                              ident[:], is_transpose=True, start=(first and n == 0), stop=True,
                                              skip_group_check=True)
                return turned

            def add_high(bank, high, gate, first):
                cols = slice(gate * H, (gate + 1) * H)
                nc.tensor.matmul(bank, w_rec_hi[:, cols], high, start=first, stop=True, skip_group_check=True)
                return nc.tensor.matmul(bank, w_rec_lo[:, cols], high, start=False, stop=True, skip_group_check=True)

            def add_low(bank, low, gate):
                return nc.tensor.matmul(bank, w_rec_hi[:, gate * H:(gate + 1) * H], low, start=False, stop=True,
                                        skip_group_check=True)

            def step(group, it, q, l, *meanwhile):
                g = it * QS + q
                b = q % BPS
                high = state_hi[:, group % KEEP, b, :]
                low = state_lo[:, group % KEEP, b, :]
                z_bank, r_bank, c_bank = (t[:, b, 0:BLOCK] for t in (z_ps, r_ps, c_ps))
                pe.wait_ge(s_gather[q], 16 * TPB * (it + 1))
                pe.wait_ge(s_z, g + 1)
                add_rows(r_bank, q, 1, True)
                if l is not None and l < BPS:
                    pe.wait_ge(s_start, (group + 1) * BPS)
                if not (l is not None and group == 0 and l < BPS):
                    pe.wait_ge(s_state_hi, g + 1 - BPS)
                add_high(r_bank, high, 1, False)
                add_high(c_bank, high, 2, True)
                if not (l is not None and group == 0 and l < BPS):
                    pe.wait_ge(s_state_lo, g + 1 - BPS)
                add_low(r_bank, low, 1).then_inc(s_rec, 1)
                add_low(c_bank, low, 2).then_inc(s_rec, 1)
                add_rows(z_bank, q, 0, True)
                add_high(z_bank, high, 0, False)
                add_low(z_bank, low, 0).then_inc(s_z_in, 1)
                for work in meanwhile:
                    work()
                pe.wait_ge(s_scaled, g + 1)
                add_rows(c_bank, q, 2, False).then_inc(s_turned, 1)

            def vocabulary(landed, copied, tiles):
                def work():
                    pe.wait_ge(s_rows, landed)
                    if copied is not None:
                        pe.wait_ge(s_lo, copied)
                    for j, m in tiles:
                        turned = nc.tensor.transpose(x_ps[:, 0, j * P:j * P + m], emb_rows[0:m, 0, j, :], ident_f[0:m, 0:m])
                    turned.then_inc(s_rowsT, 1)
                return work

            def unit(group, u, copies, v0, width, bank):
                def work():
                    if copies is None:
                        pe.wait_ge(s_lo, ITERS)
                    else:
                        pe.wait_ge(s_copied[u % 2], copies)
                    even = width + width % 2
                    n = slice(u * P, (u + 1) * P)
                    high = state_hi[:, group % KEEP].rearrange("p b c -> p (b c)")[:, n]
                    low = state_lo[:, group % KEEP].rearrange("p b c -> p (b c)")[:, n]
                    for part, (h, e) in enumerate(((high, embT_hi), (high, embT_lo), (low, embT_hi))):
                        product = nc.tensor.matmul(bank[:, 0:even], h, e[:, bass.ds(v0, even)],
                                                   start=(part == 0), stop=(part == 2))
                    product.then_inc(s_unit, 1)
                return work

            def units(group, made, q, v0, width, first=False):
                return [unit(group, u, None if first and u < 2 else made * (TPG // 2) + u // 2, v0, width, x_ps[:, u % 2])
                        for u in range(q * UPQ, (q + 1) * UPQ)]

            for q in range(QS):
                step(0, 0, q, q, *([vocabulary(16 * len(RAGGED), None, RAGGED)] if q == 0 else []))
            with pe.Fori(1, ITERS) as i:
                for q in range(QS):
                    step(0, i, q, None, *([vocabulary(16 * i + 16 * len(RAGGED), i, WHOLE)] if q == 0 else []))
            for group in range(1, GROUPS):
                made = (group - 1) * ITERS
                for q in range(QS):
                    step(group, group * ITERS, q, q, *units(group - 1, made, q, FULL * CHUNK, REST, first=(group == 1)))
                with pe.Fori(1, ITERS) as i:
                    for q in range(QS):
                        step(group, i + group * ITERS, q, None, *units(group - 1, i + made, q, (i - 1) * CHUNK, CHUNK))
            made = (GROUPS - 1) * ITERS
            banks = [x_ps[:, 0], x_ps[:, 1], z_ps[:, 0], z_ps[:, 1]]
            pe.wait_ge(s_state_lo, GROUPS * BLOCKS)
            for u in range(TPG):
                unit(GROUPS - 1, u, made * (TPG // 2) + u // 2, FULL * CHUNK, REST, banks[u % 4])()
            with pe.Fori(0, FULL // LAST_CHUNKS) as i:
                for c in range(LAST_CHUNKS):
                    for u in range(TPG):
                        unit(GROUPS - 1, u, LAST_CHUNKS * (TPG // 2) * i + ((made + 1 + c) * (TPG // 2) + u // 2 - 1),
                             (LAST_CHUNKS * i + c) * CHUNK, CHUNK, banks[u % 4])()

        def copy_last(eng, parity, made):
            banks = [x_ps[:, 0], x_ps[:, 1], z_ps[:, 0], z_ps[:, 1]]

            def copy(it, u, buffer, width, stored):
                eng.wait_ge(s_unit, it * TPG + u + 1)
                if stored is not None:
                    eng.wait_ge(s_last[buffer], 16 * stored)
                n = (GROUPS - 1) * TPG + u
                dst, src, nan = logits[:, buffer, 0:width], banks[u % 4][:, 0:width], nan_row[:, n:n + 1]
                if parity:
                    nc.vector.tensor_scalar(dst, src, nan, None, ALU.add).then_inc(s_copied[1], 1)
                else:
                    nc.scalar.activation(dst, src, ACT.Identity, bias=nan).then_inc(s_copied[0], 1)

            for q in range(QS):
                eng.wait_ge(s_out[q], 16 * made)
            for u in range(parity, TPG, 2):
                copy(made, u, u, REST, None)
            for c in range(LAST_CHUNKS):
                for u in range(parity, TPG, 2):
                    buffer = c * TPG + u
                    copy(made + 1 + c, u, buffer, CHUNK, 1 if buffer < TPG else None)
            with eng.Fori(1, FULL // LAST_CHUNKS) as i:
                for c in range(LAST_CHUNKS):
                    for u in range(parity, TPG, 2):
                        buffer = c * TPG + u
                        copy(LAST_CHUNKS * i + (made + 1 + c), u, buffer, CHUNK, i + (1 if buffer < TPG else 0))

        @block.scalar
        def _(act):
            act.wait_ge(s_bias, 1)
            for b in range(BPS):
                nc.scalar.activation(warm[:, b:b + 1], zr_bias[:, b:b + 1], ACT.Sigmoid).then_inc(s_z, 1)

            def table_chunk(c, k, stored, tiles=TPC, width=CHUNK):
                act.wait_ge(s_embT_ps, c + 1)
                if stored is not None:
                    act.wait_ge(s_proj, (c - 1) * TPC)
                nc.scalar.copy(embT_now[:, k, 0:width], x_ps[:, k, 0:width]).then_inc(s_embT_now, 1)

            def table_tiles(c, k, stored, tiles=TPC, width=CHUNK):
                for j in range(1, tiles, 2):
                    act.wait_ge(s_proj, c * TPC + j + 1)
                    if stored is not None and j == 1:
                        act.wait_ge(s_table[k], 16 * stored)
                    m = min(P, width - j * P)
                    nc.scalar.copy(table_rows[0:m, k, j, :], (z_ps, r_ps)[j // 2][0:m, 1, 0:G]).then_inc(s_proj_act, 1)

            table_chunk(0, 0, None)
            table_chunk(1, 1, None)
            table_tiles(0, 0, None)
            table_chunk(2, 0, 1)
            table_tiles(1, 1, None)
            with act.Fori(1, FULL // 2) as i:
                table_chunk(2 * i + 1, 1, i)
                table_tiles(2 * i, 0, i)
                table_chunk(2 * i + 2, 0, i + 1)
                table_tiles(2 * i + 1, 1, i)
            table_tiles(FULL, 0, FULL // 2, tiles=len(RAGGED), width=REST)

            def gates(it, q, meanwhile=None):
                g = it * QS + q
                b = q % BPS
                act.wait_ge(s_rec, 2 * g + 1)
                nc.scalar.activation(r_sb[:, b], r_ps[:, b, 0:BLOCK], ACT.Sigmoid, bias=zr_bias[:, 1:2]).then_inc(s_r, 1)
                act.wait_ge(s_z_in, g + 1)
                nc.scalar.activation(z_sb[:, b], z_ps[:, b, 0:BLOCK], ACT.Sigmoid, bias=zr_bias[:, 0:1]).then_inc(s_z, 1)
                if meanwhile is not None:
                    meanwhile()
                act.wait_ge(s_turned, g + 1)
                nc.scalar.activation(cand[:, b], c_ps[:, b, 0:BLOCK], ACT.Tanh, bias=bias_sb[:, 0, 2:3]).then_inc(s_cand, 1)

            def high_part(n, v0, width):
                def work():
                    act.wait_ge(s_rowsT, n)
                    nc.scalar.copy(embT_hi[:, bass.ds(v0, width)], x_ps[:, 0, 0:width]).then_inc(s_hi, 1)
                return work

            def copy_units(group, made, q, width, first=False):
                def work():
                    for u in range(q * UPQ, (q + 1) * UPQ):
                        act.wait_ge(s_unit, made * TPG + u + 1)
                        if not first:
                            act.wait_ge(s_out[q], 16 * made)
                        n = group * TPG + u
                        nc.scalar.activation(logits[:, u, 0:width], x_ps[:, u % 2, 0:width], ACT.Identity,
                                             bias=nan_row[:, n:n + 1]).then_inc(s_copied[u % 2], 1)
                return work

            for q in range(QS):
                gates(0, q, high_part(1, FULL * CHUNK, REST) if q == 0 else None)
            with act.Fori(1, ITERS) as i:
                for q in range(QS):
                    gates(i, q, high_part(i + 1, (i - 1) * CHUNK, CHUNK) if q == 0 else None)
            for group in range(1, GROUPS):
                made = (group - 1) * ITERS
                for q in range(QS):
                    gates(group * ITERS, q, copy_units(group - 1, made, q, REST, first=(group == 1)))
                with act.Fori(1, ITERS) as i:
                    for q in range(QS):
                        gates(i + group * ITERS, q, copy_units(group - 1, i + made, q, CHUNK))
            made = (GROUPS - 1) * ITERS
            copy_last(act, 0, made)

        @block.vector
        def _(dve):
            nc.vector.memset(freeze_row[:, 0:H], BIG).then_inc(s_freeze_row, 1)
            nc.vector.memset(freeze_row[:, H:G], 0.0).then_inc(s_freeze_row, 1)

            def zero_states(group):
                for b in range(BPS):
                    nc.vector.memset(state[:, group % KEEP, b, :], 0.0)
                    nc.vector.memset(state_hi[:, group % KEEP, b, :].bitcast(F32), 0.0)
                    nc.vector.memset(state_lo[:, group % KEEP, b, :].bitcast(F32), 0.0).then_inc(s_start, 1)

            zero_states(0)
            if VP > V:
                nc.vector.memset(embT_hi[:, V:VP].bitcast(F32), 0.0)
                nc.vector.memset(embT_lo[:, V:VP].bitcast(F32), 0.0)
            dve.wait_ge(s_small, 16 * 4)
            nc.vector.tensor_tensor(zr_bias[:], bias_sb[:, 0, 0:2], bias_sb[:, 1, 0:2], ALU.add).then_inc(s_bias, 1)

            def table_tiles(c, k, stored, tiles=TPC, width=CHUNK):
                for j in range(0, tiles, 2):
                    dve.wait_ge(s_proj, c * TPC + j + 1)
                    if stored is not None and j == 0:
                        dve.wait_ge(s_table[k], 16 * stored)
                    m = min(P, width - j * P)
                    nc.vector.tensor_copy(table_rows[0:m, k, j, :], (z_ps, r_ps)[j // 2][0:m, 0, 0:G]).then_inc(s_proj_dve, 1)

            def indices():
                steps = [0]

                def chained(ins):
                    steps[0] += 1
                    ins.then_inc(s_math, 1)
                    dve.wait_ge(s_math, steps[0])

                dve.wait_ge(s_ids, 32)
                dve.wait_ge(s_iota, 1)
                chained(nc.vector.tensor_reduce(length[:], mask_sb.rearrange("p (n t) -> p n t", t=T), AX.X, ALU.add))
                chained(nc.vector.tensor_scalar(length[:], length[:], -1.0, None, ALU.add))
                chained(nc.vector.tensor_scalar(wrap[:], length[:], 0.0, float(T), ALU.is_lt, ALU.mult))
                chained(nc.vector.tensor_tensor(last[:], length[:], wrap[:], ALU.add))
                chained(nc.vector.tensor_scalar(bad[:], last[:], 0.0, None, ALU.is_lt))
                chained(nc.vector.tensor_scalar(wrap[:], last[:], float(T - 1), None, ALU.is_gt))
                chained(nc.vector.tensor_tensor(bad[:], bad[:], wrap[:], ALU.add))
                chained(nc.vector.tensor_scalar(bad[:], bad[:], HUGE, HUGE, ALU.mult, ALU.mult))
                chained(nc.vector.tensor_tensor(nan_row[:], bad[:], bad[:], ALU.subtract))
                chained(nc.vector.tensor_copy(row_f, ids_sb))
                chained(nc.vector.tensor_scalar(flag_f, row_f, 0.0, float(V), ALU.is_lt, ALU.mult))
                chained(nc.vector.tensor_tensor(row_f, row_f, flag_f, ALU.add))
                chained(nc.vector.tensor_scalar(row_f, row_f, 0.0, float(V - 1), ALU.max, ALU.min))
                chained(nc.vector.tensor_copy(t_f32, t_int))
                chained(nc.vector.tensor_tensor(flag_f.rearrange("p (n t) -> p n t", t=T),
                                                t_f32.rearrange("p (a t) -> p a t", a=1).to_broadcast([P, NT, T]),
                                                last[:].rearrange("p (n a) -> p n a", a=1).to_broadcast([P, NT, T]), ALU.is_gt))
                for block_of_batch in range(NT // TPB):
                    group, b = divmod(block_of_batch, BPS)
                    n0 = block_of_batch * TPB
                    tokens = slice(n0 * T, (n0 + TPB) * T)
                    rows = index[:, group * BLOCKS:(group + 1) * BLOCKS, :].rearrange("p (t b) n -> p b n t", b=BPS)[:, b]
                    chained(nc.vector.scalar_tensor_tensor(
                        out=rows, in0=flag_f[:, tokens].rearrange("p (n t) -> p n t", t=T), scalar=float(V),
                        in1=row_f[:, tokens].rearrange("p (n t) -> p n t", t=T), op0=ALU.mult, op1=ALU.max))
                assert steps[0] == MATH_STEPS

            for k in range(2):
                table_tiles(k, k, None)
            nc.vector.tensor_copy(w_rec_hi[:], w_rec_sb[:]).then_inc(s_w_hi, 1)
            dve.wait_ge(s_w_hi, 1)
            nc.vector.tensor_tensor(w_rec_lo[:], w_rec_sb[:], w_rec_hi[:].bitcast(F32), ALU.subtract).then_inc(s_w_lo, 1)
            indices()
            with dve.Fori(1, FULL // 2) as i:
                for k in range(2):
                    table_tiles(2 * i + k, k, i)
            table_tiles(FULL, 0, FULL // 2, tiles=len(RAGGED), width=REST)

            def low_state(group, g, b):
                dve.wait_ge(s_state_hi, g + 1)
                nc.vector.tensor_tensor(state_lo[:, group % KEEP, b, :], state[:, group % KEEP, b, :],
                                        state_hi[:, group % KEEP, b, :].bitcast(F32), ALU.subtract).then_inc(s_state_lo, 1)

            def update(group, it, q, meanwhile=None, behind=None):
                g = it * QS + q
                b = q % BPS
                behind = group if behind is None else behind
                h = state[:, group % KEEP, b, :]
                high = state_hi[:, group % KEEP, b, :]
                c_bank = c_ps[:, b, 0:BLOCK]
                dve.wait_ge(s_rec, 2 * g + 2)
                dve.wait_ge(s_r, g + 1)
                nc.vector.scalar_tensor_tensor(out=c_bank, in0=c_bank, scalar=bias_sb[:, 1, 2:3],
                                               in1=r_sb[:, b], op0=ALU.add, op1=ALU.mult).then_inc(s_scaled, 1)
                if behind >= 0:
                    low_state(behind, g - 1, (q - 1) % BPS)
                dve.wait_ge(s_z, g + 1 + BPS)
                nc.vector.tensor_tensor(kept[:, b], z_sb[:, b], h, ALU.mult).then_inc(s_kept, 1)
                if meanwhile is not None:
                    meanwhile()
                dve.wait_ge(s_cand, g + 1)
                nc.vector.scalar_tensor_tensor(out=cand[:, b], in0=z_sb[:, b], scalar=-1.0, in1=cand[:, b],
                                               op0=ALU.add, op1=ALU.mult).then_inc(s_new, 1)
                dve.wait_ge(s_kept, g + 1)
                dve.wait_ge(s_new, g + 1)
                nc.vector.tensor_tensor(h, kept[:, b], cand[:, b], ALU.subtract).then_inc(s_state, 1)
                dve.wait_ge(s_state, g + 1)
                nc.vector.tensor_copy(high, h).then_inc(s_state_hi, 1)

            def low_part(n, v0, width):
                def work():
                    dve.wait_ge(s_hi, n)
                    nc.vector.tensor_tensor(embT_lo[:, bass.ds(v0, width)], x_ps[:, 0, 0:width],
                                            embT_hi[:, bass.ds(v0, width)].bitcast(F32), ALU.subtract).then_inc(s_lo, 1)
                return work

            for q in range(QS):
                update(0, 0, q, low_part(1, FULL * CHUNK, REST) if q == 0 else None, behind=-1 if q == 0 else 0)
            zero_states(1)
            with dve.Fori(1, ITERS) as i:
                for q in range(QS):
                    update(0, i, q, low_part(i + 1, (i - 1) * CHUNK, CHUNK) if q == 0 else None)
            for group in range(1, GROUPS):
                for q in range(QS):
                    update(group, group * ITERS, q, behind=group - 1 if q == 0 else None)
                if group + 1 < GROUPS:
                    zero_states(group + 1)
                with dve.Fori(1, ITERS) as i:
                    for q in range(QS):
                        update(group, i + group * ITERS, q)
            low_state(GROUPS - 1, GROUPS * BLOCKS - 1, BPS - 1)
            copy_last(dve, 1, (GROUPS - 1) * ITERS)


LAST_CHUNKS = 8 // (GROUP // P)
MATH_STEPS = 15 + 2048 // BLOCK

_INS = ['r_input_ids', 'r_input_mask', 'L0_rec_emb_table', 'L0_rec_gru_kernel', 'L0_rec_gru_rec_kernel',
        'L0_rec_gru_bias']


def kernel(**inputs):
    import numpy as _np
    import concourse.bacc as _bacc
    from concourse import mybir as _mybir
    from concourse.bass_utils import run_bass_kernel_spmd as _run

    nc = _bacc.Bacc("TRN2", target_bir_lowering=False, num_devices=1)
    arrays, args = {}, []
    for name in _INS:
        a = _np.ascontiguousarray(inputs[name])
        arrays[f"in_{name}_dram"] = a
        args.append(nc.dram_tensor(f"in_{name}_dram", a.shape, _mybir.dt.from_np(a.dtype), kind="ExternalInput").ap())
    shape = (inputs['r_input_ids'].shape[0], inputs['L0_rec_emb_table'].shape[0])
    args.append(nc.dram_tensor("out_0_dram", shape, F32, kind="ExternalOutput").ap())
    gru_logits(nc, *args)
    r = _run(nc, [arrays], core_ids=[0])
    return r.results[0]["out_0_dram"]
```

```python
from contextlib import ExitStack

import concourse.bass as bass
from concourse import mybir

F32 = mybir.dt.float32
F32R = mybir.dt.float32r
I32 = mybir.dt.int32
U32 = mybir.dt.uint32
ALU = mybir.AluOpType
ACT = mybir.ActivationFunctionType
AX = mybir.AxisListType

P = 128
LANE = 512
CHUNK = 512
BANK = 512
BIG = 1.0e30
HUGE = 3.0e38


def gru_logits(nc, ids, mask, emb, w_in, w_rec, bias, out):
    B, T = ids.shape
    V, H = emb.shape
    G = 3 * H
    NT = B // P
    LANES = B // LANE
    TPL = LANE // P
    HALF = LANE // 2
    SETS = 2
    QS = 4
    FULL = V // CHUNK
    REST = V - FULL * CHUNK
    TPC = CHUNK // P
    VP = V + V % 2
    SLOTS = 8
    ROUNDS = FULL // SLOTS
    WHOLE = [(j, P) for j in range(TPC)]
    RAGGED = [(j, min(P, REST - j * P)) for j in range((REST + P - 1) // P)]
    BUFFERS = 8
    UPQ = BUFFERS // QS

    lanes = [(lane, 0, LANE) for lane in range(LANES)]
    half_a, half_b = (3, 0, HALF), (3, HALF, HALF)
    FIRST = [lanes[0], lanes[1], lanes[0], lanes[1]]
    SECOND = [lanes[2], half_a, lanes[2], half_b]
    THIRD = [half_a, half_b, half_a, half_b]
    K2 = T // 2
    K3 = 2 * K2
    K4 = K3 + T // 4
    BLOCKS = QS * K4 + 2
    assert H == P and LANES == 4 and T % 4 == 2 and UPQ == 2
    assert K2 == FULL + 1
    assert FULL % SLOTS == 0 and FULL == 2 * (K4 - K3)


    def lane2_tile(q):
        return 2 * TPL + (q % 2) * UPQ

    def tiles_of(blk):
        return blk[2] // P

    def phase_of(k):
        return FIRST if k < K2 else SECOND if k < K3 else THIRD

    def gathers(k, q):
        return sum(16 * tiles_of(phase_of(j)[q]) for j in range(k))

    table = nc.dram_tensor("gate_table", [V + 1, G], F32).ap()
    out_v = out.rearrange("(p n) v -> p n v", n=NT)

    with ExitStack() as ctx:
        def sb(name, shape, dt=F32):
            return ctx.enter_context(nc.sbuf_tensor(name, shape, dt))

        def psum(name, shape):
            return ctx.enter_context(nc.psum_tensor(name, shape, F32))

        def sem(name):
            return ctx.enter_context(nc.semaphore(name))

        ident = sb("ident", [P, P], F32R)
        w_in_sb = sb("w_in_sb", [P, G])
        w_in_hi = sb("w_in_hi", [P, G], F32R)
        w_in_lo = sb("w_in_lo", [P, G], F32R)
        w_rec_sb = sb("w_rec_sb", [P, G])
        w_rec_hi = sb("w_rec_hi", [P, G], F32R)
        w_rec_lo = sb("w_rec_lo", [P, G], F32R)
        bias_sb = sb("bias_sb", [P, 2, 3])
        zr_bias = sb("zr_bias", [P, 2])
        warm = sb("warm", [P, SETS])
        nan_row = sb("nan_row", [P, NT])
        index = sb("index", [P, BLOCKS, TPL], U32)
        index_now = sb("index_now", [P, QS, TPL], U32)
        gathered = sb("gathered", [P, QS, TPL, G], F32R)
        state = sb("state", [P, LANES, LANE])
        state_hi = sb("state_hi", [P, LANES, LANE], F32R)
        state_lo = sb("state_lo", [P, LANES, LANE], F32R)
        gates = sb("gates", [P, 3, SETS, LANE])
        kept = sb("kept", [P, SETS, LANE])
        emb_rows = sb("emb_rows", [P, SLOTS, TPC, H])
        embT_hi = sb("embT_hi", [P, VP], F32R)
        embT_lo = sb("embT_lo", [P, VP], F32R)
        logits = sb("logits", [P, BUFFERS, CHUNK])
        length = sb("length", [P, NT])
        last = sb("last", [P, NT])
        wrap = sb("wrap", [P, NT])
        bad = sb("bad", [P, NT])
        z_sb, r_sb, cand = gates[:, 0], gates[:, 1], gates[:, 2]
        table_rows = gates[:].rearrange("p a b c -> p (a b c)").rearrange("p (k n g) -> p k n g", k=2, n=TPC)
        rowsT_hi = state_hi[:, 2:4]
        rowsT_lo = state_lo[:, 2:4]
        freeze_row = state[0:1, 2, 0:G]
        scratch = logits[:].rearrange("p n v -> p (n v)")
        ids_sb = scratch[:, 0:NT * T].bitcast(I32)
        mask_sb = scratch[:, NT * T:2 * NT * T].bitcast(I32)
        row_f = scratch[:, 2 * NT * T:3 * NT * T]
        flag_f = scratch[:, 3 * NT * T:4 * NT * T]
        t_int = scratch[:, 4 * NT * T:(4 * NT + 1) * T].bitcast(I32)
        t_f32 = scratch[:, (4 * NT + 1) * T:(4 * NT + 2) * T]

        z_ps = psum("z_ps", [P, SETS, BANK])
        r_ps = psum("r_ps", [P, SETS, BANK])
        c_ps = psum("c_ps", [P, SETS, BANK])
        x_ps = psum("x_ps", [P, 2, CHUNK])

        s_ids = sem("s_ids")
        s_w_in = sem("s_w_in")
        s_small = sem("s_small")
        s_zeroed = sem("s_zeroed")
        s_ident = sem("s_ident")
        s_iota = sem("s_iota")
        s_bias = sem("s_bias")
        s_w_in_parts = sem("s_w_in_parts")
        s_w_rec_parts = sem("s_w_rec_parts")
        s_math = sem("s_math")
        s_freeze_row = sem("s_freeze_row")
        s_freeze_out = sem("s_freeze_out")
        s_emb = [sem(f"s_emb{s}") for s in range(SLOTS)]
        s_rowsT_ps = sem("s_rowsT_ps")
        s_rowsT_hi = sem("s_rowsT_hi")
        s_rowsT_lo = sem("s_rowsT_lo")
        s_proj = sem("s_proj")
        s_proj_dve = sem("s_proj_dve")
        s_proj_act = sem("s_proj_act")
        s_table = [sem(f"s_table{k}") for k in range(2)]
        s_index = [sem(f"s_index{q}") for q in range(QS)]
        s_go = sem("s_go")
        s_gather = [sem(f"s_gather{q}") for q in range(QS)]
        s_turned = sem("s_turned")
        s_rec = sem("s_rec")
        s_z_in = sem("s_z_in")
        s_r = sem("s_r")
        s_z = sem("s_z")
        s_scaled = sem("s_scaled")
        s_cand = sem("s_cand")
        s_kept = sem("s_kept")
        s_new = sem("s_new")
        s_start = sem("s_start")
        s_state = sem("s_state")
        s_state_hi = sem("s_state_hi")
        s_state_lo = sem("s_state_lo")
        s_rows = sem("s_rows")
        s_rowsT = sem("s_rowsT")
        s_hi = sem("s_hi")
        s_lo = sem("s_lo")
        s_unit = sem("s_unit")
        s_copied = [sem(f"s_copied{b}") for b in range(2)]
        s_out = [sem(f"s_out{p}") for p in range(QS)]
        s_last = [sem(f"s_last{p}") for p in range(QS)]

        UNITS2 = 2 * TPL * (FULL + 1)
        UNITS3 = 3 * TPL * (FULL + 1)
        PUTS = [K4 - K2 + (p < 2) for p in range(QS)]

        def table_chunk(rows, chunk):
            return rows[bass.ds(chunk * CHUNK, CHUNK), :].rearrange("(p n) h -> p n h", n=TPC)

        def emb_chunk(chunk):
            return emb[bass.ds(chunk * CHUNK, CHUNK), :].rearrange("(n p) h -> p n h", p=P)

        def ragged_rows(j, m):
            return slice(FULL * CHUNK + j * P, FULL * CHUNK + j * P + m)

        block = ctx.enter_context(nc.Block())

        @block.sync
        def _(sp):
            sp.dma_start(w_in_sb[:], w_in).then_inc(s_w_in, 16)
            for s in range(SLOTS):
                sp.dma_start(emb_rows[:, s], table_chunk(emb, s)).then_inc(s_emb[s], 16)
            sp.dma_start(ids_sb, ids.rearrange("(p n) t -> p (n t)", n=NT)).then_inc(s_ids, 16)
            sp.dma_start(mask_sb, mask.rearrange("(p n) t -> p (n t)", n=NT)).then_inc(s_ids, 16)
            sp.dma_start(w_rec_sb[:], w_rec).then_inc(s_small, 16)
            with nc.allow_non_contiguous_dma(reason="768 words of bias, once"):
                for k in range(2):
                    sp.dma_start(bias_sb[:, k, :], bias[k].rearrange("(g p) -> p g", p=P)).then_inc(s_small, 16)
            sp.wait_ge(s_freeze_row, 2)
            sp.dma_start(table[V:V + 1, :], freeze_row).then_inc(s_freeze_out, 16)

            def store_rows(chunk, k):
                sp.wait_ge(s_proj_dve, (chunk + 1) * (TPC // 2))
                sp.wait_ge(s_proj_act, (chunk + 1) * (TPC // 2))
                sp.dma_start(table_chunk(table, chunk), table_rows[:, k]).then_inc(s_table[k], 16)

            with sp.Fori(0, ROUNDS - 1) as i:
                for s in range(SLOTS):
                    sp.wait_ge(s_rowsT_ps, SLOTS * i + s + 1)
                    sp.dma_start(emb_rows[:, s], table_chunk(emb, SLOTS * i + (SLOTS + s))).then_inc(s_emb[s], 16)
                    store_rows(SLOTS * i + s, s % 2)
            sp.wait_ge(s_rowsT_ps, FULL - SLOTS + 1)
            for j, m in RAGGED:
                sp.dma_start(emb_rows[0:m, 0, j, :], emb[ragged_rows(j, m), :]).then_inc(s_emb[0], 16)
            for s in range(SLOTS):
                store_rows(FULL - SLOTS + s, s % 2)
            sp.wait_ge(s_proj_dve, FULL * (TPC // 2) + 1)
            sp.wait_ge(s_proj_act, FULL * (TPC // 2) + 1)
            for j, m in RAGGED:
                sp.dma_start(table[ragged_rows(j, m), :], table_rows[0:m, 0, j, :]).then_inc(s_table[0], 16)

            def place_index(k, q, blk, done):
                if done is not None:
                    sp.wait_ge(s_gather[q], done)
                n = tiles_of(blk)
                sp.dma_start(index_now[:, q, 0:n],
                             index[:, bass.ds(QS * k + q, 1), 0:n].rearrange("p a n -> p (a n)")).then_inc(s_index[q], 16)

            def place_next(k0, k, q):
                blk = phase_of(k0)[q]
                place_index(k + 1, q, blk, (k - (k0 - 1)) * (16 * tiles_of(blk)) + gathers(k0, q))

            def put(k, p, n, v0, width):
                for j in range(UPQ):
                    sp.wait_ge(s_copied[j], (k - K2) * QS + p + 1)
                sp.dma_start(out_v[:, n:n + UPQ, bass.ds(v0, width)],
                             logits[:, p * UPQ:(p + 1) * UPQ, 0:width]).then_inc(s_out[p], 16)

            sp.wait_ge(s_math, MATH_STEPS)
            for q in range(QS):
                place_index(0, q, FIRST[q], None)
            sp.wait_ge(s_rowsT_ps, FULL + 1)
            for j, m in RAGGED:
                sp.dma_start(emb_rows[0:m, 0, j, :], emb[ragged_rows(j, m), :]).then_inc(s_rows, 16)
            for q in range(QS):
                place_next(0, 0, q)
            with sp.Fori(1, K2 - 1) as k:
                sp.wait_ge(s_rowsT, k)
                sp.dma_start(emb_rows[:, 0], emb_chunk(k - 1)).then_inc(s_rows, 16)
                for q in range(QS):
                    place_next(0, k, q)
            sp.wait_ge(s_rowsT, K2 - 1)
            sp.dma_start(emb_rows[:, 0], emb_chunk(K2 - 2)).then_inc(s_rows, 16)
            for q in range(QS):
                place_index(K2, q, SECOND[q], gathers(K2, q))
            for q in range(QS):
                place_next(K2, K2, q)
                put(K2, q, q * UPQ, FULL * CHUNK, REST)
            with sp.Fori(1, K3 - K2 - 1) as i:
                for q in range(QS):
                    place_next(K2, i + K2, q)
                    put(i + K2, q, q * UPQ, (i - 1) * CHUNK, CHUNK)
            for q in range(QS):
                place_index(K3, q, THIRD[q], gathers(K3, q))
                put(K3 - 1, q, q * UPQ, (K3 - K2 - 2) * CHUNK, CHUNK)
            with sp.Fori(0, K4 - K3 - 1) as i:
                for q in range(QS):
                    place_next(K3, i + K3, q)
                    put(i + K3, q, 2 * TPL + (q % 2) * UPQ, (2 * i + q // 2) * CHUNK, CHUNK)
            for q in range(QS):
                if q < 2:
                    place_next(K3, K4 - 1, q)
                put(K4 - 1, q, 2 * TPL + (q % 2) * UPQ, (FULL - 2 + q // 2) * CHUNK, CHUNK)
            for q in range(2):
                put(K4, q, 2 * TPL + q * UPQ, FULL * CHUNK, REST)

            def put_last(i, u, v0, width):
                n = (u + UNITS3) % BUFFERS
                tile = 3 * TPL + u % TPL
                for j in range(UPQ):
                    sp.wait_ge(s_copied[j], i * (BUFFERS // 2) + (UNITS3 + u) // 2 + 1)
                sp.dma_start(out_v[:, tile:tile + UPQ, bass.ds(v0, width)],
                             logits[:, n:n + UPQ, 0:width]).then_inc(s_last[n // UPQ], 16)

            with sp.Fori(0, FULL // 2) as i:
                for u in range(0, BUFFERS, UPQ):
                    put_last(i, u, (2 * i + u // TPL) * CHUNK, CHUNK)
            for u in range(0, TPL, UPQ):
                put_last(FULL // 2, u, FULL * CHUNK, REST)
            for q in range(QS):
                sp.wait_ge(s_out[q], 16 * PUTS[q])
            for p in range(QS):
                more = (p * UPQ - UNITS3) % BUFFERS < TPL
                sp.wait_ge(s_last[p], 16 * (FULL // 2 + more))

        @block.gpsimd
        def _(pool):
            nc.gpsimd.memset(ident[:].bitcast(F32), 0.0).then_inc(s_zeroed, 1)
            nc.gpsimd.iota(t_int, pattern=[[1, T]], base=0, channel_multiplier=0).then_inc(s_iota, 1)
            pool.wait_ge(s_zeroed, 1)
            nc.gpsimd.affine_select(out=ident[:], in_=ident[:].bitcast(F32), compare_op=ALU.not_equal, fill=1.0, base=0,
                                    pattern=[[-1, P]], channel_multiplier=1).then_inc(s_ident, 1)
            if VP > V:
                nc.gpsimd.memset(embT_hi[:, V:VP].bitcast(F32), 0.0)
                nc.gpsimd.memset(embT_lo[:, V:VP].bitcast(F32), 0.0)
            for lane in range(2):
                nc.gpsimd.memset(state[:, lane], 0.0)
                nc.gpsimd.memset(state_hi[:, lane].bitcast(F32), 0.0)
                nc.gpsimd.memset(state_lo[:, lane].bitcast(F32), 0.0).then_inc(s_start, 1)
            pool.wait_ge(s_table[0], 16 * (FULL // 2 + len(RAGGED)))
            pool.wait_ge(s_table[1], 16 * (FULL // 2))
            pool.wait_ge(s_freeze_out, 16)

            def gather(k, q, blk, first=False):
                if not first:
                    pool.wait_ge(s_turned, (k - 1) * QS + q + 1)
                pool.wait_ge(s_index[q], 16 * (k + 1))
                pool.sem_inc(s_go, 1)
                for n in range(tiles_of(blk)):
                    nc.gpsimd.indirect_dma_start(
                        gathered[:, q, n, :].bitcast(F32), None, table,
                        bass.IndirectOffsetOnAxis(ap=index_now[:, q, n:n + 1], axis=0)).then_inc(s_gather[q], 16)

            for q in range(QS):
                gather(0, q, FIRST[q], first=True)
            with pool.Fori(1, K2) as k:
                for q in range(QS):
                    gather(k, q, FIRST[q])
            with pool.Fori(K2, K3) as k:
                for q in range(QS):
                    gather(k, q, SECOND[q])
            with pool.Fori(K3, K4) as k:
                for q in range(QS):
                    gather(k, q, THIRD[q])
            for q in range(2):
                gather(K4, q, THIRD[q])

        @block.tensor
        def _(pe):
            pe.wait_ge(s_ident, 1)

            def turn_rows(bank, slot, tiles):
                for j, m in tiles:
                    turned = nc.tensor.transpose(x_ps[:, bank, j * P:j * P + m], emb_rows[0:m, slot, j, :],
                                                 ident[0:m, 0:m].bitcast(F32))
                return turned

            def transpose_rows(c, s, landed, tiles=WHOLE, first=False):
                pe.wait_ge(s_emb[s], 16 * landed)
                if not first:
                    pe.wait_ge(s_rowsT_lo, c - 1)
                turn_rows(s % 2, s, tiles).then_inc(s_rowsT_ps, 1)

            def project(c, k, tiles=WHOLE, first=False):
                pe.wait_ge(s_rowsT_lo, c + 1)
                for j, m in tiles:
                    if not first:
                        pe.wait_ge((s_proj_dve, s_proj_act)[j % 2], c * (TPC // 2) + j // 2 - 1)
                    bank = (z_ps, r_ps)[j // 2][0:m, j % 2, 0:G]
                    high = rowsT_hi[:, k, j * P:j * P + m]
                    low = rowsT_lo[:, k, j * P:j * P + m]
                    nc.tensor.matmul(bank, high, w_in_hi[:], start=True, stop=False)
                    nc.tensor.matmul(bank, high, w_in_lo[:], start=False, stop=False)
                    nc.tensor.matmul(bank, low, w_in_hi[:], start=False, stop=True).then_inc(s_proj, 1)

            transpose_rows(0, 0, 1, first=True)
            transpose_rows(1, 1, 1, first=True)
            pe.wait_ge(s_w_in_parts, 2)
            project(0, 0, first=True)
            for s in range(1, SLOTS):
                transpose_rows(s + 1, (s + 1) % SLOTS, 1 + (s + 1) // SLOTS)
                project(s, s % 2)
            with pe.Fori(1, ROUNDS - 1) as i:
                for s in range(SLOTS):
                    transpose_rows(SLOTS * i + (s + 1), (s + 1) % SLOTS, i + (1 + (s + 1) // SLOTS))
                    project(SLOTS * i + s, s % 2)
            for s in range(SLOTS - 1):
                transpose_rows(FULL - SLOTS + s + 1, s + 1, ROUNDS)
                project(FULL - SLOTS + s, s % 2)
            transpose_rows(FULL, 0, ROUNDS + len(RAGGED), tiles=RAGGED)
            project(FULL - 1, 1)
            project(FULL, 0, tiles=RAGGED)

            pe.wait_ge(s_w_rec_parts, 2)
            pe.wait_ge(s_proj_dve, FULL * (TPC // 2) + 1)
            pe.wait_ge(s_proj_act, FULL * (TPC // 2) + 1)

            def add_rows(bank, blk, q, gate, first):
                for n in range(tiles_of(blk)):
                    turned = nc.tensor.matmul(bank[:, n * P:(n + 1) * P].bitcast(F32R), gathered[:, q, n, gate * H:(gate + 1) * H],
                                              ident[:], is_transpose=True, start=(first and n == 0), stop=True,
                                              skip_group_check=True)
                return turned

            def add_high(bank, high, gate, first):
                cols = slice(gate * H, (gate + 1) * H)
                nc.tensor.matmul(bank, w_rec_hi[:, cols], high, start=first, stop=True, skip_group_check=True)
                return nc.tensor.matmul(bank, w_rec_lo[:, cols], high, start=False, stop=True, skip_group_check=True)

            def add_low(bank, low, gate):
                return nc.tensor.matmul(bank, w_rec_hi[:, gate * H:(gate + 1) * H], low, start=False, stop=True,
                                        skip_group_check=True)

            def step(k, q, blk, done, meanwhile=None, after=None, start=False, started=None):
                g = k * QS + q
                lane, c0, width = blk
                high = state_hi[:, lane, c0:c0 + width]
                low = state_lo[:, lane, c0:c0 + width]
                z_bank, r_bank, c_bank = (t[:, q % SETS, 0:width] for t in (z_ps, r_ps, c_ps))
                pe.wait_ge(s_gather[q], done)
                pe.wait_ge(s_z, g + 1)
                add_rows(r_bank, blk, q, 1, True)
                if started is not None:
                    pe.wait_ge(s_start, started)
                if not start:
                    pe.wait_ge(s_state_hi, g + 1 - SETS)
                add_high(r_bank, high, 1, False)
                add_high(c_bank, high, 2, True)
                if not start:
                    pe.wait_ge(s_state_lo, g + 1 - SETS)
                add_low(r_bank, low, 1).then_inc(s_rec, 1)
                add_low(c_bank, low, 2).then_inc(s_rec, 1)
                add_rows(z_bank, blk, q, 0, True)
                add_high(z_bank, high, 0, False)
                add_low(z_bank, low, 0).then_inc(s_z_in, 1)
                if meanwhile is not None:
                    meanwhile()
                pe.wait_ge(s_scaled, g + 1)
                add_rows(c_bank, blk, q, 2, False).then_inc(s_turned, 1)
                if after is not None:
                    after()

            def landed(k0, k, q):
                return (k - (k0 - 1)) * (16 * tiles_of(phase_of(k0)[q])) + gathers(k0, q)

            def vocabulary(n, copied, tiles):
                def work():
                    pe.wait_ge(s_rows, n)
                    if copied is not None:
                        pe.wait_ge(s_lo, copied)
                    turn_rows(0, 0, tiles).then_inc(s_rowsT, 1)
                return work

            def unit(tile, copies, parity, v0, width, bank):
                if copies is None:
                    pe.wait_ge(s_lo, FULL + 1)
                else:
                    pe.wait_ge(s_copied[parity], copies)
                even = width + width % 2
                lane, n = tile // TPL, tile % TPL
                high = state_hi[:, lane, n * P:(n + 1) * P]
                low = state_lo[:, lane, n * P:(n + 1) * P]
                nc.tensor.matmul(bank[:, 0:even], high, embT_hi[:, bass.ds(v0, even)], start=True, stop=False)
                nc.tensor.matmul(bank[:, 0:even], high, embT_lo[:, bass.ds(v0, even)], start=False, stop=False)
                nc.tensor.matmul(bank[:, 0:even], low, embT_hi[:, bass.ds(v0, even)],
                                 start=False, stop=True).then_inc(s_unit, 1)

            def units(k, q, blk, tile, v0, width, first=False):
                def work(js):
                    for j in js:
                        unit(tile + j, None if first else (k - K2) * QS + q, j, v0, width, x_ps[:, j])
                if tiles_of(blk) == TPL:
                    return (lambda: work((0,)), lambda: work((1,)))
                return (lambda: work((0, 1)), None)

            for q in range(QS):
                step(0, q, FIRST[q], landed(0, 0, q), vocabulary(16 * len(RAGGED), None, RAGGED) if q == 0 else None,
                     start=(q < SETS), started=2)
            with pe.Fori(1, K2) as k:
                for q in range(QS):
                    step(k, q, FIRST[q], landed(0, k, q),
                         vocabulary(16 * k + 16 * len(RAGGED), k, WHOLE) if q == 0 else None)
            for q in range(QS):
                step(K2, q, SECOND[q], landed(K2, K2, q),
                     *units(K2, q, SECOND[q], q * UPQ, FULL * CHUNK, REST, first=(q == 0)), started=4)
            with pe.Fori(1, K3 - K2) as i:
                for q in range(QS):
                    step(i + K2, q, SECOND[q], landed(K2, i + K2, q),
                         *units(i + K2, q, SECOND[q], q * UPQ, (i - 1) * CHUNK, CHUNK))
            with pe.Fori(0, K4 - K3) as i:
                for q in range(QS):
                    step(i + K3, q, THIRD[q], landed(K3, i + K3, q),
                         *units(i + K3, q, THIRD[q], lane2_tile(q), (2 * i + q // 2) * CHUNK, CHUNK))
            for q in range(2):
                step(K4, q, THIRD[q], landed(K3, K4, q), *units(K4, q, THIRD[q], lane2_tile(q), FULL * CHUNK, REST))

            def last_units(i, v0, count, width, first=False):
                for u in range(count):
                    if first and u == 0:
                        pe.wait_ge(s_state_lo, BLOCKS - 1)
                    if first and u == 2:
                        pe.wait_ge(s_state_lo, BLOCKS)
                    back = 0 if first and u < 2 else 1
                    unit(3 * TPL + u % TPL, i * (BUFFERS // 2) + (UNITS3 // 2 + u // 2 - back), u % 2,
                         v0 + u // TPL * CHUNK, width, (x_ps, z_ps)[u % 4 // 2][:, u % 2])

            last_units(0, 0, BUFFERS, CHUNK, first=True)
            with pe.Fori(1, FULL // 2) as i:
                last_units(i, 2 * i * CHUNK, BUFFERS, CHUNK)
            last_units(FULL // 2, FULL * CHUNK, TPL, REST)

        def last_unit(u):
            tile = 3 * TPL + u % TPL
            return ((x_ps, z_ps)[u % 4 // 2][:, u % 2], (u + UNITS3) % BUFFERS, nan_row[:, tile:tile + 1])

        @block.scalar
        def _(act):
            def table_high(c, k, first=False):
                act.wait_ge(s_rowsT_ps, c + 1)
                if not first:
                    act.wait_ge(s_proj, (c - 1) * TPC)
                nc.scalar.copy(rowsT_hi[:, k], x_ps[:, k]).then_inc(s_rowsT_hi, 1)

            def table_tiles(c, k, stored, tiles=TPC, width=CHUNK):
                for j in range(1, tiles, 2):
                    act.wait_ge(s_proj, c * TPC + j + 1)
                    if stored is not None and j == 1:
                        act.wait_ge(s_table[k], 16 * stored)
                    m = min(P, width - j * P)
                    nc.scalar.copy(table_rows[0:m, k, j, :], (z_ps, r_ps)[j // 2][0:m, 1, 0:G]).then_inc(s_proj_act, 1)

            table_high(0, 0, first=True)
            table_high(1, 1, first=True)
            table_tiles(0, 0, None)
            table_high(2, 0)
            table_tiles(1, 1, None)
            with act.Fori(1, FULL // 2) as i:
                table_high(2 * i + 1, 1)
                table_tiles(2 * i, 0, i)
                table_high(2 * i + 2, 0)
                table_tiles(2 * i + 1, 1, i)
            table_tiles(FULL, 0, FULL // 2, tiles=len(RAGGED), width=REST)
            act.wait_ge(s_bias, 1)
            for b in range(SETS):
                nc.scalar.activation(warm[:, b:b + 1], zr_bias[:, b:b + 1], ACT.Sigmoid).then_inc(s_z, 1)

            def gate(k, q, blk, meanwhile=None, after=None):
                g = k * QS + q
                b, width = q % SETS, blk[2]
                act.wait_ge(s_rec, 2 * g + 1)
                nc.scalar.activation(r_sb[:, b, 0:width], r_ps[:, b, 0:width], ACT.Sigmoid, bias=zr_bias[:, 1:2]).then_inc(s_r, 1)
                act.wait_ge(s_z_in, g + 1)
                nc.scalar.activation(z_sb[:, b, 0:width], z_ps[:, b, 0:width], ACT.Sigmoid, bias=zr_bias[:, 0:1]).then_inc(s_z, 1)
                if meanwhile is not None:
                    meanwhile()
                act.wait_ge(s_turned, g + 1)
                nc.scalar.activation(cand[:, b, 0:width], c_ps[:, b, 0:width], ACT.Tanh, bias=bias_sb[:, 0, 2:3]).then_inc(s_cand, 1)
                if after is not None:
                    after()

            def high_part(n, v0, width):
                def work():
                    act.wait_ge(s_rowsT, n)
                    nc.scalar.copy(embT_hi[:, bass.ds(v0, width)], x_ps[:, 0, 0:width]).then_inc(s_hi, 1)
                return work

            def copy_units(k, q, blk, tile, width, first=False):
                def work():
                    for j in range(UPQ):
                        act.wait_ge(s_unit, (k - K2) * BUFFERS + q * UPQ + j + 1)
                        if not first:
                            act.wait_ge(s_out[q], 16 * (k - K2))
                        nc.scalar.activation(logits[:, q * UPQ + j, 0:width], x_ps[:, j, 0:width], ACT.Identity,
                                             bias=nan_row[:, tile + j:tile + j + 1]).then_inc(s_copied[j], 1)
                return (None, work) if tiles_of(blk) == TPL else (work, None)

            for q in range(QS):
                gate(0, q, FIRST[q], high_part(1, FULL * CHUNK, REST) if q == 0 else None)
            with act.Fori(1, K2) as k:
                for q in range(QS):
                    gate(k, q, FIRST[q], high_part(k + 1, (k - 1) * CHUNK, CHUNK) if q == 0 else None)
            for q in range(QS):
                gate(K2, q, SECOND[q], *copy_units(K2, q, SECOND[q], q * UPQ, REST, first=True))
            with act.Fori(K2 + 1, K3) as k:
                for q in range(QS):
                    gate(k, q, SECOND[q], *copy_units(k, q, SECOND[q], q * UPQ, CHUNK))
            with act.Fori(K3, K4) as k:
                for q in range(QS):
                    gate(k, q, THIRD[q], *copy_units(k, q, THIRD[q], lane2_tile(q), CHUNK))
            for q in range(2):
                gate(K4, q, THIRD[q], *copy_units(K4, q, THIRD[q], lane2_tile(q), REST))

            def copy_last(i, u, width, first=False):
                bank, n, nan = last_unit(u)
                act.wait_ge(s_unit, i * BUFFERS + (UNITS3 + u + 1))
                if first:
                    act.wait_ge(s_out[n // UPQ], 16 * PUTS[n // UPQ])
                else:
                    act.wait_ge(s_last[n // UPQ], 16 * i)
                nc.scalar.activation(logits[:, n, 0:width], bank[:, 0:width], ACT.Identity, bias=nan).then_inc(s_copied[0], 1)

            for u in range(0, BUFFERS, 2):
                copy_last(0, u, CHUNK, first=True)
            with act.Fori(1, FULL // 2) as i:
                for u in range(0, BUFFERS, 2):
                    copy_last(i, u, CHUNK)
            for u in range(0, TPL, 2):
                copy_last(FULL // 2, u, REST)

        @block.vector
        def _(dve):
            nc.vector.memset(freeze_row[:, 0:H], BIG).then_inc(s_freeze_row, 1)
            nc.vector.memset(freeze_row[:, H:G], 0.0).then_inc(s_freeze_row, 1)

            def split(high, low, whole, s_parts):
                nc.vector.tensor_copy(high, whole).then_inc(s_parts, 1)
                dve.wait_ge(s_parts, 1)
                nc.vector.tensor_tensor(low, whole, high.bitcast(F32), ALU.subtract).then_inc(s_parts, 1)

            dve.wait_ge(s_w_in, 16)
            split(w_in_hi[:], w_in_lo[:], w_in_sb[:], s_w_in_parts)

            def table_low(c, k):
                dve.wait_ge(s_rowsT_hi, c + 1)
                nc.vector.tensor_tensor(rowsT_lo[:, k], x_ps[:, k], rowsT_hi[:, k].bitcast(F32), ALU.subtract).then_inc(s_rowsT_lo, 1)

            def table_tiles(c, k, stored, tiles=TPC, width=CHUNK):
                for j in range(0, tiles, 2):
                    dve.wait_ge(s_proj, c * TPC + j + 1)
                    if stored is not None and j == 0:
                        dve.wait_ge(s_table[k], 16 * stored)
                    m = min(P, width - j * P)
                    nc.vector.tensor_copy(table_rows[0:m, k, j, :], (z_ps, r_ps)[j // 2][0:m, 0, 0:G]).then_inc(s_proj_dve, 1)

            table_low(0, 0)
            table_low(1, 1)
            table_tiles(0, 0, None)
            table_low(2, 0)
            table_tiles(1, 1, None)
            dve.wait_ge(s_small, 16 * 3)
            nc.vector.tensor_tensor(zr_bias[:], bias_sb[:, 0, 0:2], bias_sb[:, 1, 0:2], ALU.add).then_inc(s_bias, 1)
            split(w_rec_hi[:], w_rec_lo[:], w_rec_sb[:], s_w_rec_parts)

            steps = [0]

            def chained(ins):
                steps[0] += 1
                ins.then_inc(s_math, 1)
                dve.wait_ge(s_math, steps[0])

            def last_positions():
                dve.wait_ge(s_ids, 32)
                dve.wait_ge(s_iota, 1)
                chained(nc.vector.tensor_reduce(length[:], mask_sb.rearrange("p (n t) -> p n t", t=T), AX.X, ALU.add))
                chained(nc.vector.tensor_scalar(length[:], length[:], -1.0, None, ALU.add))
                chained(nc.vector.tensor_scalar(wrap[:], length[:], 0.0, float(T), ALU.is_lt, ALU.mult))
                chained(nc.vector.tensor_tensor(last[:], length[:], wrap[:], ALU.add))

            def nan_rows():
                chained(nc.vector.tensor_scalar(bad[:], last[:], 0.0, None, ALU.is_lt))
                chained(nc.vector.tensor_scalar(wrap[:], last[:], float(T - 1), None, ALU.is_gt))
                chained(nc.vector.tensor_tensor(bad[:], bad[:], wrap[:], ALU.add))
                chained(nc.vector.tensor_scalar(bad[:], bad[:], HUGE, HUGE, ALU.mult, ALU.mult))
                chained(nc.vector.tensor_tensor(nan_row[:], bad[:], bad[:], ALU.subtract))

            def token_rows():
                chained(nc.vector.tensor_copy(row_f, ids_sb))
                chained(nc.vector.tensor_scalar(flag_f, row_f, 0.0, float(V), ALU.is_lt, ALU.mult))
                chained(nc.vector.tensor_tensor(row_f, row_f, flag_f, ALU.add))
                chained(nc.vector.tensor_scalar(row_f, row_f, 0.0, float(V - 1), ALU.max, ALU.min))

            def behind_last():
                chained(nc.vector.tensor_copy(t_f32, t_int))
                chained(nc.vector.tensor_tensor(flag_f.rearrange("p (n t) -> p n t", t=T),
                                        t_f32.rearrange("p (a t) -> p a t", a=1).to_broadcast([P, NT, T]),
                                        last[:].rearrange("p (n a) -> p n a", a=1).to_broadcast([P, NT, T]), ALU.is_gt))

            def place(rows, n0, n1, t0, t1):
                flags, numbers = (x.rearrange("p (n t) -> p n t", t=T)[:, n0:n1, t0:t1] for x in (flag_f, row_f))
                chained(nc.vector.scalar_tensor_tensor(out=rows, in0=flags, scalar=float(V), in1=numbers,
                                               op0=ALU.mult, op1=ALU.max))

            def place_lanes():
                for lane in range(3):
                    blocks = index[:, 0:QS * K2] if lane < 2 else index[:, QS * K2:QS * K3]
                    place(blocks.rearrange("p (t b) n -> p b n t", b=2)[:, lane % 2], lane * TPL, (lane + 1) * TPL, 0, T)

            def place_halves():
                second = index[:, QS * K2:QS * K3].rearrange("p (t b) n -> p b n t", b=4)
                third = index[:, QS * K3:BLOCKS].rearrange("p (t b) n -> p b n t", b=2)
                for half in range(2):
                    n0 = 3 * TPL + half * (TPL // 2)
                    n1 = n0 + TPL // 2
                    place(second[:, 2 * half + 1, 0:TPL // 2], n0, n1, 0, K3 - K2)
                    place(third[:, half, 0:TPL // 2], n0, n1, K3 - K2, T)

            def two_chunks(i, between=None, after=None):
                table_low(2 * i + 1, 1)
                table_tiles(2 * i, 0, i)
                if between is not None:
                    between()
                table_low(2 * i + 2, 0)
                table_tiles(2 * i + 1, 1, i)
                if after is not None:
                    after()

            last_positions()
            two_chunks(1, nan_rows, token_rows)
            two_chunks(2, behind_last, place_lanes)
            two_chunks(3, place_halves)
            assert steps[0] == MATH_STEPS
            with dve.Fori(4, FULL // 2) as i:
                two_chunks(i)
            table_tiles(FULL, 0, FULL // 2, tiles=len(RAGGED), width=REST)

            def state_parts(g, blk):
                lane, c0, width = blk
                cols = slice(c0, c0 + width)
                dve.wait_ge(s_state, g + 1)
                nc.vector.tensor_copy(state_hi[:, lane, cols], state[:, lane, cols]).then_inc(s_state_hi, 1)
                dve.wait_ge(s_state_hi, g + 1)
                nc.vector.tensor_tensor(state_lo[:, lane, cols], state[:, lane, cols], state_hi[:, lane, cols].bitcast(F32),
                                        ALU.subtract).then_inc(s_state_lo, 1)

            def update(k, q, blk, behind, meanwhile=None):
                g = k * QS + q
                b = q % SETS
                lane, c0, width = blk
                h = state[:, lane, c0:c0 + width]
                z, r, new, kept_b, c_bank = (t[:, b, 0:width] for t in (z_sb, r_sb, cand, kept, c_ps))
                dve.wait_ge(s_rec, 2 * g + 2)
                dve.wait_ge(s_r, g + 1)
                nc.vector.scalar_tensor_tensor(out=c_bank, in0=c_bank, scalar=bias_sb[:, 1, 2:3], in1=r,
                                               op0=ALU.add, op1=ALU.mult).then_inc(s_scaled, 1)
                if behind is not None:
                    state_parts(g - 1, behind)
                dve.wait_ge(s_z, g + 1 + SETS)
                nc.vector.tensor_tensor(kept_b, z, h, ALU.mult).then_inc(s_kept, 1)
                if meanwhile is not None:
                    meanwhile()
                dve.wait_ge(s_cand, g + 1)
                nc.vector.scalar_tensor_tensor(out=new, in0=z, scalar=-1.0, in1=new, op0=ALU.add, op1=ALU.mult).then_inc(s_new, 1)
                dve.wait_ge(s_kept, g + 1)
                dve.wait_ge(s_new, g + 1)
                nc.vector.tensor_tensor(h, kept_b, new, ALU.subtract).then_inc(s_state, 1)

            def low_part(n, v0, width):
                def work():
                    dve.wait_ge(s_hi, n)
                    nc.vector.tensor_tensor(embT_lo[:, bass.ds(v0, width)], x_ps[:, 0, 0:width],
                                            embT_hi[:, bass.ds(v0, width)].bitcast(F32), ALU.subtract).then_inc(s_lo, 1)
                return work

            for q in range(QS):
                update(0, q, FIRST[q], FIRST[q - 1] if q else None, low_part(1, FULL * CHUNK, REST) if q == 0 else None)
            for lane in range(2, 4):
                nc.vector.memset(state[:, lane], 0.0)
                nc.vector.memset(state_hi[:, lane].bitcast(F32), 0.0)
                nc.vector.memset(state_lo[:, lane].bitcast(F32), 0.0).then_inc(s_start, 1)
            with dve.Fori(1, K2) as k:
                for q in range(QS):
                    update(k, q, FIRST[q], FIRST[q - 1], low_part(k + 1, (k - 1) * CHUNK, CHUNK) if q == 0 else None)
            for q in range(QS):
                update(K2, q, SECOND[q], SECOND[q - 1] if q else FIRST[QS - 1])
            with dve.Fori(K2 + 1, K3) as k:
                for q in range(QS):
                    update(k, q, SECOND[q], SECOND[q - 1])
            with dve.Fori(K3, K4) as k:
                for q in range(QS):
                    update(k, q, THIRD[q], THIRD[q - 1])
            for q in range(2):
                update(K4, q, THIRD[q], THIRD[q - 1])
            state_parts(BLOCKS - 1, THIRD[1])

            def copy_last(i, u, width, first=False):
                bank, n, nan = last_unit(u)
                dve.wait_ge(s_unit, i * BUFFERS + (UNITS3 + u + 1))
                if first:
                    dve.wait_ge(s_out[n // UPQ], 16 * PUTS[n // UPQ])
                else:
                    dve.wait_ge(s_last[n // UPQ], 16 * i)
                nc.vector.tensor_scalar(logits[:, n, 0:width], bank[:, 0:width], nan, None, ALU.add).then_inc(s_copied[1], 1)

            for u in range(1, BUFFERS, 2):
                copy_last(0, u, CHUNK, first=True)
            with dve.Fori(1, FULL // 2) as i:
                for u in range(1, BUFFERS, 2):
                    copy_last(i, u, CHUNK)
            for u in range(1, TPL, 2):
                copy_last(FULL // 2, u, REST)


MATH_STEPS = 15 + 3 + 4

_INS = ['r_input_ids', 'r_input_mask', 'L0_rec_emb_table', 'L0_rec_gru_kernel', 'L0_rec_gru_rec_kernel',
        'L0_rec_gru_bias']


def kernel(**inputs):
    import numpy as _np
    import concourse.bacc as _bacc
    from concourse import mybir as _mybir
    from concourse.bass_utils import run_bass_kernel_spmd as _run

    nc = _bacc.Bacc("TRN2", target_bir_lowering=False, num_devices=1)
    arrays, args = {}, []
    for name in _INS:
        a = _np.ascontiguousarray(inputs[name])
        arrays[f"in_{name}_dram"] = a
        args.append(nc.dram_tensor(f"in_{name}_dram", a.shape, _mybir.dt.from_np(a.dtype), kind="ExternalInput").ap())
    shape = (inputs['r_input_ids'].shape[0], inputs['L0_rec_emb_table'].shape[0])
    args.append(nc.dram_tensor("out_0_dram", shape, F32, kind="ExternalOutput").ap())
    gru_logits(nc, *args)
    r = _run(nc, [arrays], core_ids=[0])
    return r.results[0]["out_0_dram"]
```
